# Optimizing a Trainium2 kernel written in Bass

```python
import numpy as np
import jax
import jax.numpy as jnp

def _softmax(x, axis=-1):
    return jax.nn.softmax(x, axis=axis)

def _gelu(x):
    return jax.nn.gelu(x, approximate=True)

def _silu(x):
    return jax.nn.silu(x)

def _sigmoid(x):
    return jax.nn.sigmoid(x)

def _layernorm(x, axis=-1, eps=1e-05):
    m = jnp.mean(x, axis=axis, keepdims=True)
    v = jnp.var(x, axis=axis, keepdims=True)
    return (x - m) / jnp.sqrt(v + eps)

def _scatter_add(tgt, idx, src, axis=0):
    return tgt.at[idx].add(src)

def _segment_sum(src, seg, n):
    return jax.ops.segment_sum(src, seg, n)
kernel_name = 'mk_seq_postln_d1_jaxref_r8_d99791'

def setup_inputs(seed: int=0):
    np.random.seed(seed)
    _w = jnp.asarray

    def _L0_attn_setup():
        import jax, jax.numpy as jnp
        import numpy as np
        D_MODEL = 128
        N_HEADS = 16
        HEAD_DIM = D_MODEL // N_HEADS
        SCALE = HEAD_DIM ** (-0.5)
        MIN_VAL = jnp.finfo(jnp.float32).min

        def _split_heads(y):
            B, T, _ = y.shape
            return y.reshape(B, T, N_HEADS, HEAD_DIM).transpose(0, 2, 1, 3)
        key = jax.random.key(seed)
        ks = jax.random.split(key, 7)
        B, T = (1, 256)
        s = D_MODEL ** (-0.5)
        return {'x': jax.random.normal(ks[0], (B, T, D_MODEL), dtype=jnp.float32), 'Wq': jax.random.normal(ks[1], (D_MODEL, D_MODEL), dtype=jnp.float32) * s, 'Wk1': jax.random.normal(ks[2], (D_MODEL, D_MODEL), dtype=jnp.float32) * s, 'Wk2': jax.random.normal(ks[3], (D_MODEL, D_MODEL), dtype=jnp.float32) * s, 'Wv': jax.random.normal(ks[4], (D_MODEL, D_MODEL), dtype=jnp.float32) * s, 'Wo': jax.random.normal(ks[5], (D_MODEL, D_MODEL), dtype=jnp.float32) * s, 'lambda_logit': jnp.zeros((N_HEADS,), dtype=jnp.float32)}
    _L0_attn_in = _L0_attn_setup()

    def _L0_ffn_setup():
        import jax, jax.numpy as jnp
        import numpy as np
        E = 8
        K = 2
        D = 128
        H = 4 * D
        EPS = 1e-05
        TEMP = 1.5
        key = jax.random.key(seed)
        ks = jax.random.split(key, 6)
        B, T = (2, 256)
        x = jax.random.normal(ks[0], (B, T, D), dtype=jnp.float32)
        gamma = jnp.ones((D,), dtype=jnp.float32)
        beta = jnp.zeros((D,), dtype=jnp.float32)
        router_w = jax.random.normal(ks[1], (E, D), dtype=jnp.float32) * 0.02
        W1 = jax.random.normal(ks[2], (E, D, H), dtype=jnp.float32) * 0.02
        W2 = jax.random.normal(ks[3], (E, H, D), dtype=jnp.float32) * 0.02
        return {'x': x, 'gamma': gamma, 'beta': beta, 'router_w': router_w, 'W1': W1, 'W2': W2}
    _L0_ffn_in = _L0_ffn_setup()
    _d = {'L0_attn_x': _L0_attn_in['x'], 'L0_attn_Wq': _L0_attn_in['Wq'], 'L0_attn_Wk1': _L0_attn_in['Wk1'], 'L0_attn_Wk2': _L0_attn_in['Wk2'], 'L0_attn_Wv': _L0_attn_in['Wv'], 'L0_attn_Wo': _L0_attn_in['Wo'], 'L0_attn_lambda_logit': _L0_attn_in['lambda_logit'], 'L0_ffn_gamma': _L0_ffn_in['gamma'], 'L0_ffn_beta': _L0_ffn_in['beta'], 'L0_ffn_router_w': _L0_ffn_in['router_w'], 'L0_ffn_W1': _L0_ffn_in['W1'], 'L0_ffn_W2': _L0_ffn_in['W2']}
    _x0 = _d['L0_attn_x']
    _d['L0_attn_x'] = jax.random.normal(jax.random.fold_in(jax.random.key(seed), 1), (8, 512, 128), dtype=_x0.dtype)
    del _x0
    return _d

def reference(L0_attn_x, L0_attn_Wq, L0_attn_Wk1, L0_attn_Wk2, L0_attn_Wv, L0_attn_Wo, L0_attn_lambda_logit, L0_ffn_gamma, L0_ffn_beta, L0_ffn_router_w, L0_ffn_W1, L0_ffn_W2):

    def _L0_attn_ref(x, Wq, Wk1, Wk2, Wv, Wo, lambda_logit):
        import jax, jax.numpy as jnp
        import numpy as np
        D_MODEL = 128
        N_HEADS = 16
        HEAD_DIM = D_MODEL // N_HEADS
        SCALE = HEAD_DIM ** (-0.5)
        MIN_VAL = jnp.finfo(jnp.float32).min

        def _split_heads(y):
            B, T, _ = y.shape
            return y.reshape(B, T, N_HEADS, HEAD_DIM).transpose(0, 2, 1, 3)
        B, T, _ = x.shape
        q = _split_heads(x @ Wq.T)
        k1 = _split_heads(x @ Wk1.T)
        k2 = _split_heads(x @ Wk2.T)
        v = _split_heads(x @ Wv.T)
        s1 = jnp.einsum('bhqd,bhkd->bhqk', q, k1) * SCALE
        s2 = jnp.einsum('bhqd,bhkd->bhqk', q, k2) * SCALE
        causal = jnp.arange(T)[None, :] <= jnp.arange(T)[:, None]
        s1 = jnp.where(causal[None, None], s1, MIN_VAL)
        s2 = jnp.where(causal[None, None], s2, MIN_VAL)
        attn_exp = jax.nn.softmax(s1, axis=-1)
        attn_noise = jax.nn.softmax(s2, axis=-1)
        lam = jax.nn.sigmoid(lambda_logit)[None, :, None, None]
        attn = attn_exp - lam * attn_noise
        denom = jnp.maximum(jnp.sum(jnp.abs(attn), axis=-1, keepdims=True), 1e-06)
        attn = attn / denom
        out = jnp.einsum('bhqk,bhkd->bhqd', attn, v)
        out = out.transpose(0, 2, 1, 3).reshape(B, T, D_MODEL)
        return out @ Wo.T

    def _L0_ffn_ref(x, gamma, beta, router_w, W1, W2):
        import jax, jax.numpy as jnp
        import numpy as np
        E = 8
        K = 2
        D = 128
        H = 4 * D
        EPS = 1e-05
        TEMP = 1.5
        res = x
        mu = jnp.mean(x, axis=-1, keepdims=True)
        var = jnp.mean(jnp.square(x - mu), axis=-1, keepdims=True)
        xn = (x - mu) * jax.lax.rsqrt(var + EPS) * gamma + beta
        logits = jnp.einsum('btd,ed->bte', xn, router_w)
        probs = jax.nn.softmax(logits / TEMP, axis=-1)
        w, idx = jax.lax.top_k(probs, K)
        wdense = jnp.sum(jax.nn.one_hot(idx, E, dtype=w.dtype) * w[..., None], axis=-2)
        h = jax.nn.silu(jnp.einsum('btd,edf->betf', xn, W1))
        y = jnp.einsum('betf,efd->betd', h, W2)
        out = jnp.einsum('bte,betd->btd', wdense, y)
        return out + res
    x = L0_attn_x
    x = _layernorm(x + _L0_attn_ref(x, L0_attn_Wq, L0_attn_Wk1, L0_attn_Wk2, L0_attn_Wv, L0_attn_Wo, L0_attn_lambda_logit), axis=-1)
    x = _layernorm(x + _L0_ffn_ref(x, L0_ffn_gamma, L0_ffn_beta, L0_ffn_router_w, L0_ffn_W1, L0_ffn_W2), axis=-1)
    return x

_drawn_inputs = setup_inputs


def setup_inputs(seed=0):
    import zlib

    import numpy as np

    out = dict(_drawn_inputs(seed))
    spreads = {'L0_attn_lambda_logit': (0.0, 0.8), 'L0_ffn_gamma': (1.0, 0.6), 'L0_ffn_beta': (0.0, 0.8)}
    factors = {'L0_ffn_router_w': 8.0, 'L0_ffn_W1': 8.0, 'L0_ffn_W2': 8.0}
    for name, (base, spread) in spreads.items():
        noise = np.random.default_rng([zlib.crc32(name.encode()), seed]).standard_normal(out[name].shape)
        drawn = base * np.exp(spread * noise) if base else spread * noise
        out[name] = jnp.asarray(drawn.astype(out[name].dtype))
    for name, factor in factors.items():
        out[name] = (out[name] * factor).astype(out[name].dtype)
    return out
```

```python
import concourse.bass as bass
from concourse import mybir
from contextlib import ExitStack

FP32, BF16 = mybir.dt.float32, mybir.dt.bfloat16
ALU, ACT, AX = mybir.AluOpType, mybir.ActivationFunctionType, mybir.AxisListType

B, T, D = 8, 512, 128
NH, HD = 16, 8
P = 128
NT = T // P
E, F = 8, 512
NF = F // P
UNITS = NH * NT
GROUP = 4
NG = NH // GROUP
SCALE = float(HD) ** -0.5
EPS, TEMP, DENOM_MIN = 1e-5, 1.5, 1e-6
MASKED = -1e30
CREDIT = 16
ROW = sum((t + 1) * P for t in range(NT))
OFF = [sum((s + 1) * P for s in range(t)) for t in range(NT)]

LAG_DIFF = NT
LAG_TRANS = LAG_DIFF + 1
LAG_PV = LAG_DIFF + 2
LAG_OUT = LAG_PV + 1

SIDE = {}


def _place():
    def put(slot, *task):
        SIDE.setdefault(slot, []).append(task)

    put(7, "post", "attn_T")
    put(9, "post", "out_proj")
    put(11, "post", "norm1")
    put(13, "post", "norm2")
    put(14, "post", "xn_T")
    put(15, "post", "logits")
    put(16, "post", "router_exp")
    put(17, "post", "route")
    tasks = []
    for e in range(E):
        for f in range(NF):
            tasks.append(("post", "hidden", e, f))
            if f == 1 and e:
                tasks.append(("post", "expert", e - 1))
    tasks.append(("post", "expert", E - 1))
    for n, task in enumerate(tasks):
        put(17 + n, *task)
    put(17 + len(tasks), "post", "norm3")
    put(19 + len(tasks), "post", "finish")
    for n, slot in enumerate((10, 16, 22, 28, 34)):
        put(slot, "prep", ("x_T", "proj", "proj", "proj", "values")[n], max(n - 1, 0))


_place()
POST_TASKS = [t for s in sorted(SIDE) for t in SIDE[s] if t[0] == "post"]
PREP_TASKS = [t for s in sorted(SIDE) for t in SIDE[s] if t[0] == "prep"]
PSUM_TASKS = ("attn_T", "out_proj", "xn_T", "logits", "hidden", "expert", "x_T", "proj", "values")
READ_BY_ACT = ("attn_T", "xn_T", "x_T", "values")


STORED = (0, 1, 2, 0, 1)
PARTS_STORED = 3 + 2 * len(STORED)
WINDOWS = ((0, 0, 0, 2), (2, 0, 1, 3), (5, 0, 2, 3))


class Signal:

    def __init__(self, sem, per_batch, step=1):
        self.sem, self.per, self.step = sem, per_batch, step

    def after(self, batch, n):
        value = (batch * self.per + n) * self.step + CREDIT
        return max(value, 1) if isinstance(value, int) else value


def build(nc, x, wqT, wk1T, wk2T, wvT, woT, lam, gamma, beta, rwT, w1, w2, out):
    ctx = ExitStack()
    with ctx:
        def sb(name, shape, dt=FP32):
            return ctx.enter_context(nc.sbuf_tensor(name, shape, dt))

        def pb(name, shape):
            return ctx.enter_context(nc.psum_tensor(name, shape, FP32))

        signals = []

        def signal(name, per_batch, step=1):
            signals.append(Signal(ctx.enter_context(nc.semaphore(name)), per_batch, step))
            return signals[-1]

        ident = sb("ident", [P, P])
        ident_bf = sb("ident_bf", [P, P], BF16)
        causal_bf = sb("causal_bf", [P, P], BF16)
        ones_row = sb("ones_row", [1, P])
        minus_half = sb("minus_half", [P, NT])
        eps_row = sb("eps_row", [P, NT])
        rank = sb("rank", [P, NT, E])
        lam_row = sb("lam_row", [1, NH])
        lam_all = sb("lam_all", [P, NH])
        gamma_col, beta_col = sb("gamma_col", [P, 1]), sb("beta_col", [P, 1])
        wq_sb = sb("wq_sb", [P, 3, P])
        wv_sb, wo_sb = sb("wv_sb", [P, P]), sb("wo_sb", [P, P])
        rw_sb = sb("rw_sb", [P, E])
        w1_sb = sb("w1_sb", [P, E, F])
        w2_sb = sb("w2_sb", [P, E, NF, D])

        x_in = sb("x_in", [P, NT, D])
        xT = sb("xT", [P, T])
        parts = sb("parts", [P, 3, 3, T], BF16)
        rest = sb("rest", [P, 3, T])
        v_next = sb("v_next", [P, NT, D])
        v_sb = sb("v_sb", [P, NT, D])
        scratch = nc.dram_tensor("parts_dram", [3, NH, len(STORED), HD, T], BF16).ap()
        q_stack = sb("q_stack", [P, NH, T], BF16)
        k_stack = sb("k_stack", [P, NH, T], BF16)

        neg_max = sb("neg_max", [P, 2, NT, 2])
        sums = sb("sums", [P, 4, 2, NT])
        inv_l2 = sb("inv_l2", [P, 2, NT])
        coef = sb("coef", [P, 2, NT])
        exps = sb("exps", [P, 2, 2, ROW])
        diff = sb("diff", [P, 2, ROW])
        diffT = sb("diffT", [P, 2, NT * P])
        abs_sum = sb("abs_sum", [P, 2, NT])
        guard = sb("guard", [P, NT])
        inv_den = sb("inv_den", [P, NT])
        attn = sb("attn", [P, NT, D])

        x_res = sb("x_res", [P, NT, D])
        attnT = sb("attnT", [P, T])
        r1 = sb("r1", [P, NT, D])
        x1 = sb("x1", [P, NT, D])
        xh = sb("xh", [P, NT, D])
        xnT = sb("xnT", [P, T])
        stats = sb("stats", [P, 3, NT, 6])
        mv = sb("mv", [P, 3, NT, 2])
        var_eps = sb("var_eps", [P, 3, NT])
        rstd = sb("rstd", [P, 3, NT])
        route_in = sb("route_in", [P, NT, E])
        route_max = sb("route_max", [P, NT])
        route_exp = sb("route_exp", [P, NT, E])
        route_inv = sb("route_inv", [P, NT])
        probs = sb("probs", [P, NT, E])
        top = sb("top", [P, 2, NT])
        first = sb("first", [P, 2, NT])
        hit = sb("hit", [P, 4, NT, E])
        gates = sb("gates", [P, NT, E])
        tanh_sb = sb("tanh_sb", [P, 2, T])
        hT = sb("hT", [P, 2, NF, T])
        acc = sb("acc", [P, NT, D])
        y_out = sb("y_out", [P, NT, D])

        scores = pb("scores", [P, 2, 2, 512])
        trans = pb("trans", [P, NT * P])
        heads = pb("heads", [P, NT, HD])
        side = [pb(f"side{n}", [P, 512]) for n in range(2)]

        CONSTS = 8 + E
        weights_in = ctx.enter_context(nc.semaphore("weights_in"))
        consts_made = ctx.enter_context(nc.semaphore("consts_made"))
        lam_spread = ctx.enter_context(nc.semaphore("lam_spread"))
        lam_exp = ctx.enter_context(nc.semaphore("lam_exp"))
        lam_done = ctx.enter_context(nc.semaphore("lam_done"))
        x_loaded = signal("x_loaded", 1, 16)
        prep_psum = signal("prep_psum", len(PREP_TASKS))
        xT_copied = signal("xT_copied", 1)
        hi_made = signal("hi_made", 3)
        rest_made = signal("rest_made", 3)
        mid_made = signal("mid_made", 3)
        lo_made = signal("lo_made", 3)
        parts_out = signal("parts_out", PARTS_STORED, 16)
        stack_in = [signal(f"stack_in{g}", 4 * len(WINDOWS), 16) for g in range(NG)]
        v_evacuated = signal("v_evacuated", 1)
        v_copied = signal("v_copied", 1)
        score_done = signal("score_done", UNITS)
        max_done = signal("max_done", UNITS)
        exp_done = signal("exp_done", UNITS)
        coef_done = signal("coef_done", 2 * NH)
        diff_done = signal("diff_done", UNITS)
        abs_done = signal("abs_done", UNITS)
        trans_done = signal("trans_done", UNITS)
        diffT_copied = signal("diffT_copied", UNITS)
        pv_done = signal("pv_done", UNITS)
        den_done = signal("den_done", 2 * NH)
        head_out = signal("head_out", NH)
        res_loaded = signal("res_loaded", 1, 16)
        n_post_psum = sum(t[1] in PSUM_TASKS for t in POST_TASKS)
        post_psum = signal("post_psum", n_post_psum)
        attnT_copied = signal("attnT_copied", 1)
        r1_done = signal("r1_done", 1)
        moments_done = signal("moments_done", 3)
        eps_added = signal("eps_added", 3)
        rstd_done = signal("rstd_done", 3)
        x1_done = signal("x1_done", 1)
        acc_set = signal("acc_set", 1)
        xh_done = signal("xh_done", 1)
        xnT_copied = signal("xnT_copied", 1)
        logit_step = signal("logit_step", 2)
        router_exp = signal("router_exp", 1)
        ROUTE_STEPS = 16
        route_step = signal("route_step", ROUTE_STEPS)
        tanh_done = signal("tanh_done", E * NF)
        hidden_done = signal("hidden_done", E * NF)
        expert_done = signal("expert_done", E)
        y_done = signal("y_done", 1)
        y_stored = signal("y_stored", 1, 16)

        def reader(task):
            name = task[1]
            return {
                "attn_T": (attnT_copied, 1), "out_proj": (r1_done, 1), "xn_T": (xnT_copied, 1),
                "logits": (logit_step, 2), "x_T": (xT_copied, 1), "values": (v_evacuated, 1),
                "proj": (rest_made, task[2] + 1) if name == "proj" else None,
                "hidden": (hidden_done, NF * task[2] + task[3] + 1) if name == "hidden" else None,
                "expert": (expert_done, task[2] + 1) if name == "expert" else None,
            }[name]

        order = [t for s in sorted(SIDE) for t in SIDE[s] if t[1] in PSUM_TASKS]
        bank_of = {t: n % 2 for n, t in enumerate(order)}
        psum_count = {}
        for stage in ("post", "prep"):
            for n, t in enumerate([t for t in order if t[0] == stage]):
                psum_count[t] = n + 1

        def psum_of(task):
            return post_psum if task[0] == "post" else prep_psum

        def run(engine, body):
            body(-1, ("prep",))
            body(0, ("attention", "prep"))
            with engine.Fori(1, B - 1) as b:
                body(b, ("attention", "prep", "post"))
            body(B - 1, ("attention", "post"))
            body(B, ("trail", "post"))

        def units(b, stages, slot, lag):
            u = slot - lag
            if u >= 0:
                return [(b, u)] if "attention" in stages else []
            if "trail" in stages or ("attention" in stages and not (isinstance(b, int) and b == 0)):
                return [(b - 1, u + UNITS)]
            return []

        def side_tasks(b, stages, slot):
            for task in SIDE.get(slot, []):
                if task[0] in stages:
                    yield task, (b + 1 if task[0] == "prep" else b - 1)

        def tiles(ap):
            return ap.rearrange("p (t d) -> p t d", t=NT)

        block = ctx.enter_context(nc.Block())

        @block.sync
        def _(sp):
            for dst, src in ((wq_sb[:, 0, :], wqT), (wq_sb[:, 1, :], wk1T), (wq_sb[:, 2, :], wk2T),
                             (wv_sb[:, :], wvT), (wo_sb[:, :], woT), (rw_sb[:, :], rwT),
                             (gamma_col[:, :], gamma), (beta_col[:, :], beta), (lam_row[:, :], lam),
                             (w1_sb[:, :, :], w1.rearrange("e d f -> d e f")),
                             (w2_sb[:, :, :, :], w2.rearrange("e (n f) d -> f e n d", f=P))):
                sp.dma_start(dst, src).then_inc(weights_in, 16)
            for s in signals:
                sp.sem_inc(s.sem, CREDIT)

            def rows(ap, b):
                return ap[b, :, :].rearrange("(t p) d -> p t d", p=P) if isinstance(b, int) else \
                    ap[bass.ds(b, 1), :, :].rearrange("o (t p) d -> p (o t) d", p=P)

            def body(b, stages):
                if "prep" in stages:
                    n = b + 1
                    sp.wait_ge(prep_psum.sem, prep_psum.after(n - 1, 1))
                    sp.dma_start(x_in[:, :, :], rows(x, n)).then_inc(x_loaded.sem, 16)
                if "post" in stages:
                    sp.wait_ge(r1_done.sem, r1_done.after(b - 2, 1))
                    sp.dma_start(x_res[:, :, :], rows(x, b - 1)).then_inc(res_loaded.sem, 16)
                if "prep" in stages:
                    for z in range(3):
                        sp.wait_ge(lo_made.sem, lo_made.after(n, z + 1))
                        for g in range(NG):
                            sp.wait_ge(stack_in[g].sem, stack_in[g].after(n - 1, 4 * len(WINDOWS)))
                        for slot, part in enumerate(STORED if z else STORED[:3]):
                            sp.dma_start(scratch[z, :, slot, :, :], parts[:, z, part, :]).then_inc(parts_out.sem, 16)
                    sp.wait_ge(parts_out.sem, parts_out.after(n, PARTS_STORED))
                    for g in range(NG):
                        hs = slice(g * GROUP, (g + 1) * GROUP)
                        sp.wait_ge(score_done.sem, score_done.after(n - 1, (g + 1) * GROUP * NT))

                        def stored(z, slot, count):
                            return scratch[z, hs, slot:slot + count, :, :].rearrange("h s d t -> (s d) h t")

                        for half in range(2):
                            for row, q_slot, k_slot, count in WINDOWS:
                                rows_to = slice(half * 64 + row * HD, half * 64 + (row + count) * HD)
                                sp.dma_start(q_stack[rows_to, hs, :], stored(0, q_slot, count))\
                                  .then_inc(stack_in[g].sem, 16)
                                sp.dma_start(k_stack[rows_to, hs, :], stored(1 + half, k_slot, count))\
                                  .then_inc(stack_in[g].sem, 16)
                if "post" in stages:
                    sp.wait_ge(y_done.sem, y_done.after(b - 1, 1))
                    sp.dma_start(rows(out, b - 1), y_out[:, :, :]).then_inc(y_stored.sem, 16)

            run(sp, body)
            sp.wait_ge(y_stored.sem, y_stored.after(B - 1, 1))
            sp.wait_ge(parts_out.sem, parts_out.after(B - 1, PARTS_STORED))

        @block.gpsimd
        def _(pool):
            nc.gpsimd.memset(ident[:, :], 0.0).then_inc(consts_made, 1)
            nc.gpsimd.memset(causal_bf[:, :], 0.0).then_inc(consts_made, 1)
            nc.gpsimd.memset(ones_row[:, :], 1.0).then_inc(consts_made, 1)
            nc.gpsimd.memset(minus_half[:, :], -0.5).then_inc(consts_made, 1)
            nc.gpsimd.memset(eps_row[:, :], EPS).then_inc(consts_made, 1)
            for e in range(E):
                nc.gpsimd.memset(rank[:, :, e:e + 1], float(E - e)).then_inc(consts_made, 1)
            pool.wait_ge(consts_made, CONSTS - 3)
            nc.gpsimd.affine_select(out=ident[:, :], in_=ident[:, :], compare_op=ALU.not_equal, fill=1.0,
                                    base=0, pattern=[[-1, P]], channel_multiplier=1).then_inc(consts_made, 1)
            nc.gpsimd.affine_select(out=causal_bf[:, :], in_=causal_bf[:, :], compare_op=ALU.is_ge, fill=MASKED,
                                    base=0, pattern=[[-1, P]], channel_multiplier=1).then_inc(consts_made, 1)
            pool.wait_ge(consts_made, CONSTS - 1)
            nc.gpsimd.tensor_copy(ident_bf[:, :], ident[:, :]).then_inc(consts_made, 1)

            def body(b, stages):
                for slot in range(UNITS):
                    for task, n in side_tasks(b, stages, slot):
                        name = task[1]
                        if name == "proj":
                            z = task[2]
                            pool.wait_ge(mid_made.sem, mid_made.after(n, z + 1))
                            nc.gpsimd.tensor_tensor(parts[:, z, 2, :], rest[:, z, :], parts[:, z, 1, :],
                                                    ALU.subtract).then_inc(lo_made.sem, 1)
                        if name in ("out_proj", "norm1", "norm3"):
                            i = ("out_proj", "norm1", "norm3").index(name)
                            pool.wait_ge(moments_done.sem, moments_done.after(n, i + 1))
                            nc.gpsimd.tensor_tensor(var_eps[:, i, :], mv[:, i, :, 1], eps_row[:, :], ALU.add)\
                                .then_inc(eps_added.sem, 1)
                            pool.wait_ge(eps_added.sem, eps_added.after(n, i + 1))
                            nc.gpsimd.tensor_tensor(rstd[:, i, :], var_eps[:, i, :], minus_half[:, :], ALU.pow)\
                                .then_inc(rstd_done.sem, 1)

            run(pool, body)

        @block.scalar
        def _(act):
            act.wait_ge(lam_spread, 1)
            nc.scalar.activation(lam_all[:, :], side[0][:, 0:NH], ACT.Exp, scale=-1.0).then_inc(lam_exp, 1)

            def body(b, stages):
                for slot in range(UNITS):
                    for n, u in units(b, stages, slot, 0):
                        h, t = divmod(u, NT)
                        w = (t + 1) * P
                        act.wait_ge(max_done.sem, max_done.after(n, u + 1))
                        act.wait_ge(diff_done.sem, diff_done.after(n, u + 1 - 2 * NT))
                        if t == 0:
                            act.wait_ge(head_out.sem, head_out.after(n, h - 3))
                        for k in range(2):
                            i = nc.scalar.activation(exps[:, h % 2, k, OFF[t]:OFF[t] + w], scores[:, u % 2, k, 0:w],
                                                     ACT.Exp, bias=neg_max[:, h % 2, t, k:k + 1],
                                                     accum_out=sums[:, h % 4, k, t:t + 1])
                        i.then_inc(exp_done.sem, 1)
                    for n, u in units(b, stages, slot, LAG_TRANS):
                        w = (u % NT + 1) * P
                        act.wait_ge(trans_done.sem, trans_done.after(n, u + 1))
                        act.wait_ge(pv_done.sem, pv_done.after(n, u - 1))
                        nc.scalar.activation(diffT[:, u % 2, 0:w], trans[:, 0:w], ACT.Copy)\
                            .then_inc(diffT_copied.sem, 1)
                    for task, n in side_tasks(b, stages, slot):
                        name = task[1]
                        bank = side[bank_of[task]] if task in bank_of else None
                        if name == "x_T":
                            act.wait_ge(psum_of(task).sem, psum_of(task).after(n, psum_count[task]))
                            act.wait_ge(prep_psum.sem, prep_psum.after(n - 1, len(PREP_TASKS)))
                            nc.scalar.activation(xT[:, :], bank[:, :], ACT.Copy).then_inc(xT_copied.sem, 1)
                        if name == "proj":
                            z = task[2]
                            act.wait_ge(psum_of(task).sem, psum_of(task).after(n, psum_count[task]))
                            act.wait_ge(parts_out.sem, parts_out.after(n - 1, PARTS_STORED))
                            nc.scalar.activation(parts[:, z, 0, :], bank[:, :], ACT.Copy,
                                                 scale=SCALE if z == 0 else 1.0).then_inc(hi_made.sem, 1)
                        if name == "values":
                            act.wait_ge(psum_of(task).sem, psum_of(task).after(n, psum_count[task]))
                            act.wait_ge(v_copied.sem, v_copied.after(n - 1, 1))
                            nc.scalar.activation(v_next[:, :, :], tiles(bank[:, :]), ACT.Copy)\
                                .then_inc(v_evacuated.sem, 1)
                        if name == "attn_T":
                            act.wait_ge(psum_of(task).sem, psum_of(task).after(n, psum_count[task]))
                            nc.scalar.activation(attnT[:, :], bank[:, :], ACT.Copy).then_inc(attnT_copied.sem, 1)
                        if name == "xn_T":
                            act.wait_ge(psum_of(task).sem, psum_of(task).after(n, psum_count[task]))
                            nc.scalar.activation(xnT[:, :], bank[:, :], ACT.Identity, bias=beta_col[:, 0:1],
                                                 scale=gamma_col[:, 0:1]).then_inc(xnT_copied.sem, 1)
                        if name == "router_exp":
                            act.wait_ge(logit_step.sem, logit_step.after(n, 2))
                            act.wait_ge(route_step.sem, route_step.after(n - 1, ROUTE_STEPS))
                            nc.scalar.activation(route_exp[:, :, :], route_in[:, :, :], ACT.Exp, scale=1.0 / TEMP)\
                                .then_inc(router_exp.sem, 1)
                        if name == "hidden":
                            i = NF * task[2] + task[3]
                            act.wait_ge(psum_of(task).sem, psum_of(task).after(n, psum_count[task]))
                            act.wait_ge(hidden_done.sem, hidden_done.after(n, i - 1))
                            nc.scalar.activation(tanh_sb[:, i % 2, :], bank[:, :], ACT.Tanh, scale=0.5)\
                                .then_inc(tanh_done.sem, 1)

            run(act, body)

        @block.vector
        def _(dve):
            dve.wait_ge(lam_exp, 1)
            nc.vector.tensor_scalar_add(lam_all[:, :], lam_all[:, :], 1.0).then_inc(lam_done, 1)
            dve.wait_ge(lam_done, 1)
            nc.vector.reciprocal(lam_all[:, :], lam_all[:, :]).then_inc(lam_done, 1)
            dve.wait_ge(lam_done, 2)
            dve.wait_ge(consts_made, CONSTS)

            def moments(n, i, src):
                for t in range(NT):
                    nc.vector.bn_stats(stats[:, i, t, :], src[:, t, :])
                nc.vector.drain()
                for t in range(NT):
                    last = nc.vector.bn_aggr(mv[:, i, t, :], stats[:, i, t, :])
                last.then_inc(moments_done.sem, 1)

            def normalise(n, i, dst, src):
                dve.wait_ge(rstd_done.sem, rstd_done.after(n, i + 1))
                for t in range(NT):
                    last = nc.vector.tensor_scalar(dst[:, t, :], src[:, t, :], mv[:, i, t, 0:1],
                                                   rstd[:, i, t:t + 1], ALU.subtract, ALU.mult)
                return last

            def route(n):
                count = [0]

                def step(instruction):
                    count[0] += 1
                    instruction.then_inc(route_step.sem, 1)
                    dve.wait_ge(route_step.sem, route_step.after(n, count[0]))

                def over_experts(a):
                    return a.unsqueeze(2).broadcast_to([P, NT, E])

                dve.wait_ge(router_exp.sem, router_exp.after(n, 1))
                step(nc.vector.tensor_reduce(route_inv[:, :], route_exp[:, :, :], AX.X, ALU.add))
                step(nc.vector.reciprocal(route_inv[:, :], route_inv[:, :]))
                step(nc.vector.tensor_tensor(probs[:, :, :], route_exp[:, :, :], over_experts(route_inv[:, :]), ALU.mult))
                for k in range(2):
                    left = probs if k == 0 else hit[:, 3, :, :]
                    left = left[:, :, :]
                    step(nc.vector.tensor_reduce(top[:, k, :], left, AX.X, ALU.max))
                    step(nc.vector.tensor_tensor(hit[:, 2, :, :], left, over_experts(top[:, k, :]), ALU.is_equal))
                    step(nc.vector.tensor_tensor(hit[:, 2, :, :], hit[:, 2, :, :], rank[:, :, :], ALU.mult))
                    step(nc.vector.tensor_reduce(first[:, k, :], hit[:, 2, :, :], AX.X, ALU.max))
                    step(nc.vector.tensor_tensor(hit[:, k, :, :], rank[:, :, :], over_experts(first[:, k, :]), ALU.is_equal))
                    if k == 0:
                        step(nc.vector.scalar_tensor_tensor(out=hit[:, 3, :, :], in0=hit[:, 0, :, :], scalar=-2.0,
                                                            in1=probs[:, :, :], op0=ALU.mult, op1=ALU.add))
                dve.wait_ge(expert_done.sem, expert_done.after(n - 1, E))
                return count

            def body(b, stages):
                for slot in range(UNITS):
                    for n, u in units(b, stages, slot, 0):
                        h, t = divmod(u, NT)
                        w = (t + 1) * P
                        dve.wait_ge(score_done.sem, score_done.after(n, u + 1))
                        dve.wait_ge(exp_done.sem, exp_done.after(n, u + 1 - 2 * NT))
                        nc.vector.tensor_reduce(neg_max[:, h % 2, t, :], scores[:, u % 2, :, 0:w], AX.X, ALU.max,
                                                negate=True).then_inc(max_done.sem, 1)
                    for n, u in units(b, stages, slot, LAG_OUT):
                        h, t = divmod(u, NT)
                        if t < NT - 1:
                            continue
                        dve.wait_ge(abs_done.sem, abs_done.after(n, u + 1))
                        nc.vector.scalar_tensor_tensor(out=guard[:, :], in0=sums[:, h % 4, 0, :], scalar=DENOM_MIN,
                                                       in1=abs_sum[:, h % 2, :], op0=ALU.mult, op1=ALU.max)\
                            .then_inc(den_done.sem, 1)
                        dve.wait_ge(den_done.sem, den_done.after(n, 2 * h + 1))
                        nc.vector.reciprocal(inv_den[:, :], guard[:, :]).then_inc(den_done.sem, 1)
                        dve.wait_ge(den_done.sem, den_done.after(n, 2 * h + 2))
                        dve.wait_ge(pv_done.sem, pv_done.after(n, u + 1))
                        if h == 0:
                            dve.wait_ge(post_psum.sem, post_psum.after(n - 1, 1))
                        nc.vector.scalar_tensor_tensor(out=attn[:, :, h * HD:(h + 1) * HD], in0=heads[:, :, :],
                                                       scalar=-1.0,
                                                       in1=inv_den[:, :].unsqueeze(2).broadcast_to([P, NT, HD]),
                                                       op0=ALU.mult, op1=ALU.mult).then_inc(head_out.sem, 1)
                    if slot == LAG_PV and "attention" in stages:
                        dve.wait_ge(v_evacuated.sem, v_evacuated.after(b, 1))
                        dve.wait_ge(pv_done.sem, pv_done.after(b - 1, UNITS))
                        nc.vector.tensor_copy(v_sb[:, :, :], v_next[:, :, :]).then_inc(v_copied.sem, 1)
                    for n, u in units(b, stages, slot, LAG_DIFF):
                        h, t = divmod(u, NT)
                        w = (t + 1) * P
                        at = slice(OFF[t], OFF[t] + w)
                        if t == 0:
                            dve.wait_ge(exp_done.sem, exp_done.after(n, u + NT))
                            nc.vector.reciprocal(inv_l2[:, h % 2, :], sums[:, h % 4, 1, :]).then_inc(coef_done.sem, 1)
                            dve.wait_ge(coef_done.sem, coef_done.after(n, 2 * h + 1))
                            nc.vector.scalar_tensor_tensor(out=coef[:, h % 2, :], in0=sums[:, h % 4, 0, :],
                                                           scalar=lam_all[:, h:h + 1], in1=inv_l2[:, h % 2, :],
                                                           op0=ALU.mult, op1=ALU.mult).then_inc(coef_done.sem, 1)
                            dve.wait_ge(coef_done.sem, coef_done.after(n, 2 * h + 2))
                        dve.wait_ge(trans_done.sem, trans_done.after(n, u + 1 - 2 * NT))
                        dve.wait_ge(abs_done.sem, abs_done.after(n, u + 1 - 2 * NT))
                        nc.vector.scalar_tensor_tensor(out=diff[:, h % 2, at], in0=exps[:, h % 2, 1, at],
                                                       scalar=coef[:, h % 2, t:t + 1], in1=exps[:, h % 2, 0, at],
                                                       op0=ALU.mult, op1=ALU.subtract).then_inc(diff_done.sem, 1)
                        dve.wait_ge(diff_done.sem, diff_done.after(n, u + 1))
                        nc.vector.tensor_reduce(abs_sum[:, h % 2, t:t + 1], diff[:, h % 2, at], AX.X, ALU.add,
                                                apply_absolute_value=True).then_inc(abs_done.sem, 1)
                    for task, n in side_tasks(b, stages, slot):
                        name = task[1]
                        bank = side[bank_of[task]] if task in bank_of else None
                        if name == "proj":
                            z = task[2]
                            dve.wait_ge(psum_of(task).sem, psum_of(task).after(n, psum_count[task]))
                            dve.wait_ge(hi_made.sem, hi_made.after(n, z + 1))
                            dve.wait_ge(lo_made.sem, lo_made.after(n - 1, z + 1))
                            nc.vector.scalar_tensor_tensor(out=rest[:, z, :], in0=bank[:, :],
                                                           scalar=SCALE if z == 0 else 1.0, in1=parts[:, z, 0, :],
                                                           op0=ALU.mult, op1=ALU.subtract).then_inc(rest_made.sem, 1)
                            dve.wait_ge(rest_made.sem, rest_made.after(n, z + 1))
                            nc.vector.tensor_copy(parts[:, z, 1, :], rest[:, z, :]).then_inc(mid_made.sem, 1)
                        if name == "out_proj":
                            dve.wait_ge(psum_of(task).sem, psum_of(task).after(n, psum_count[task]))
                            dve.wait_ge(res_loaded.sem, res_loaded.after(n, 1))
                            nc.vector.tensor_tensor(r1[:, :, :], tiles(bank[:, :]), x_res[:, :, :], ALU.add)\
                                .then_inc(r1_done.sem, 1)
                            dve.wait_ge(r1_done.sem, r1_done.after(n, 1))
                            moments(n, 0, r1)
                        if name == "norm1":
                            normalise(n, 0, x1, r1).then_inc(x1_done.sem, 1)
                            dve.wait_ge(x1_done.sem, x1_done.after(n, 1))
                            moments(n, 1, x1)
                        if name == "norm2":
                            nc.vector.tensor_scalar(acc[:, :, :], x1[:, :, :], 2.0, None, ALU.mult)\
                                .then_inc(acc_set.sem, 1)
                            normalise(n, 1, xh, x1).then_inc(xh_done.sem, 1)
                        if name == "logits":
                            dve.wait_ge(psum_of(task).sem, psum_of(task).after(n, psum_count[task]))
                            logits = bank[:, 0:NT * E].rearrange("p (t e) -> p t e", t=NT)
                            nc.vector.tensor_reduce(route_max[:, :], logits, AX.X, ALU.max)\
                                .then_inc(logit_step.sem, 1)
                            dve.wait_ge(logit_step.sem, logit_step.after(n, 1))
                            nc.vector.tensor_tensor(route_in[:, :, :], logits,
                                                    route_max[:, :].unsqueeze(2).broadcast_to([P, NT, E]),
                                                    ALU.subtract).then_inc(logit_step.sem, 1)
                        if name == "route":
                            count = route(n)

                            def step(instruction):
                                count[0] += 1
                                instruction.then_inc(route_step.sem, 1)
                                dve.wait_ge(route_step.sem, route_step.after(n, count[0]))
                            step(nc.vector.tensor_tensor(hit[:, 2, :, :], hit[:, 0, :, :], hit[:, 1, :, :], ALU.add))
                            nc.vector.scalar_tensor_tensor(out=gates[:, :, :], in0=hit[:, 2, :, :], scalar=0.5,
                                                           in1=probs[:, :, :], op0=ALU.mult, op1=ALU.mult)\
                                .then_inc(route_step.sem, 1)
                            count[0] += 1
                            pass
                            route_total.append(count[0])
                        if name == "hidden":
                            e, f = task[2], task[3]
                            i = NF * e + f
                            dve.wait_ge(tanh_done.sem, tanh_done.after(n, i + 1))
                            m, used = (n, e - 2) if e >= 2 else (n - 1, e + E - 2)
                            dve.wait_ge(post_psum.sem, post_psum.after(m, psum_count[("post", "expert", used)]))
                            nc.vector.scalar_tensor_tensor(out=hT[:, e % 2, f, :], in0=tanh_sb[:, i % 2, :],
                                                           scalar=1.0, in1=bank[:, :], op0=ALU.add, op1=ALU.mult)\
                                .then_inc(hidden_done.sem, 1)
                        if name == "expert":
                            e = task[2]
                            dve.wait_ge(psum_of(task).sem, psum_of(task).after(n, psum_count[task]))
                            if e == 0:
                                dve.wait_ge(route_step.sem, route_step.after(n, ROUTE_STEPS))
                                dve.wait_ge(acc_set.sem, acc_set.after(n, 1))
                            else:
                                dve.wait_ge(expert_done.sem, expert_done.after(n, e))
                            for t in range(NT):
                                last = nc.vector.scalar_tensor_tensor(
                                    out=acc[:, t, :], in0=bank[:, t * D:(t + 1) * D], scalar=gates[:, t, e:e + 1],
                                    in1=acc[:, t, :], op0=ALU.mult, op1=ALU.add)
                            last.then_inc(expert_done.sem, 1)
                        if name == "norm3":
                            dve.wait_ge(expert_done.sem, expert_done.after(n, E))
                            moments(n, 2, acc)
                        if name == "finish":
                            dve.wait_ge(y_stored.sem, y_stored.after(n - 1, 1))
                            normalise(n, 2, y_out, acc).then_inc(y_done.sem, 1)

            route_total = []
            run(dve, body)
            assert set(route_total) == {ROUTE_STEPS}, route_total

        @block.tensor
        def _(pe):
            pe.wait_ge(weights_in, 11 * 16)
            pe.wait_ge(consts_made, CONSTS)
            nc.tensor.matmul(side[0][:, 0:NH], ones_row[:, :], lam_row[:, :], start=True, stop=True)\
                .then_inc(lam_spread, 1)
            pe.wait_ge(lam_done, 2)

            def side_task(task, n, waits):
                name = task[1]
                bank = side[bank_of[task]]
                for s, m, k in waits:
                    pe.wait_ge(s.sem, s.after(m, k))
                col = slice(0, P)
                if name == "x_T":
                    pe.wait_ge(x_loaded.sem, x_loaded.after(n, 1))
                    for t in range(NT):
                        last = nc.tensor.transpose(bank[:, t * P:(t + 1) * P], x_in[:, t, :], ident[:, :])
                if name == "proj":
                    pe.wait_ge(xT_copied.sem, xT_copied.after(n, 1))
                    last = nc.tensor.matmul(bank[:, :], wq_sb[:, task[2], :], xT[:, :], start=True, stop=True)
                if name == "values":
                    pe.wait_ge(xT_copied.sem, xT_copied.after(n, 1))
                    for t in range(NT):
                        last = nc.tensor.matmul(bank[:, t * P:(t + 1) * P], xT[:, t * P:(t + 1) * P], wv_sb[:, :],
                                                start=True, stop=True)
                if name == "attn_T":
                    pe.wait_ge(head_out.sem, head_out.after(n, NH))
                    for t in range(NT):
                        last = nc.tensor.transpose(bank[:, t * P:(t + 1) * P], attn[:, t, :], ident[:, :])
                if name == "out_proj":
                    pe.wait_ge(attnT_copied.sem, attnT_copied.after(n, 1))
                    for t in range(NT):
                        last = nc.tensor.matmul(bank[:, t * P:(t + 1) * P], attnT[:, t * P:(t + 1) * P], wo_sb[:, :],
                                                start=True, stop=True)
                if name == "xn_T":
                    pe.wait_ge(xh_done.sem, xh_done.after(n, 1))
                    for t in range(NT):
                        last = nc.tensor.transpose(bank[:, t * P:(t + 1) * P], xh[:, t, :], ident[:, :])
                if name == "logits":
                    pe.wait_ge(xnT_copied.sem, xnT_copied.after(n, 1))
                    for t in range(NT):
                        last = nc.tensor.matmul(bank[:, t * E:(t + 1) * E], xnT[:, t * P:(t + 1) * P], rw_sb[:, :],
                                                start=True, stop=True)
                if name == "hidden":
                    e, f = task[2], task[3]
                    pe.wait_ge(xnT_copied.sem, xnT_copied.after(n, 1))
                    last = nc.tensor.matmul(bank[:, :], w1_sb[:, e, f * P:(f + 1) * P], xnT[:, :],
                                            start=True, stop=True)
                if name == "expert":
                    e = task[2]
                    pe.wait_ge(hidden_done.sem, hidden_done.after(n, NF * (e + 1)))
                    for t in range(NT):
                        for f in range(NF):
                            last = nc.tensor.matmul(bank[:, t * D:(t + 1) * D], hT[:, e % 2, f, t * P:(t + 1) * P],
                                                    w2_sb[:, e, f, :], start=(f == 0), stop=(f == NF - 1))
                last.then_inc((post_psum if task[0] == "post" else prep_psum).sem, 1)

            def bank_waits(b, stages):
                last = [{}, {}]
                for t in order:
                    last[bank_of[t]][t[0]] = (t, -1)
                found = {}
                for t in order:
                    if t[0] not in stages:
                        continue
                    waits = []
                    for stage, (p, shift) in last[bank_of[t]].items():
                        s, k = reader(p)
                        m = b + (1 if stage == "prep" else -1) + shift
                        m = min(m, B - 1) if isinstance(m, int) else m
                        if not (isinstance(m, int) and m < 0):
                            waits.append((s, m, k))
                    found[t] = waits
                    last[bank_of[t]] = {t[0]: (t, 0)}
                return found

            def body(b, stages):
                waits = bank_waits(b, stages)
                for slot in range(UNITS):
                    for n, u in units(b, stages, slot, 0):
                        h, t = divmod(u, NT)
                        w = (t + 1) * P
                        if u % (GROUP * NT) == 0:
                            pe.wait_ge(stack_in[h // GROUP].sem, stack_in[h // GROUP].after(n, 4 * len(WINDOWS)))
                        pe.wait_ge(exp_done.sem, exp_done.after(n, u - 1))
                        for k in range(2):
                            rows = slice(64 * k, 64 * k + 64)
                            nc.tensor.matmul(scores[:, u % 2, k, 0:w], q_stack[rows, h, t * P:(t + 1) * P],
                                             k_stack[rows, h, 0:w], start=True, stop=False)
                        for k in range(2):
                            last = nc.tensor.matmul(scores[:, u % 2, k, w - P:w], ident_bf[:, :], causal_bf[:, :],
                                                    start=False, stop=True)
                        last.then_inc(score_done.sem, 1)
                    for task, n in side_tasks(b, stages, slot):
                        if task in bank_of:
                            side_task(task, n, waits[task])
                    for n, u in units(b, stages, slot, LAG_TRANS):
                        h, t = divmod(u, NT)
                        pe.wait_ge(diff_done.sem, diff_done.after(n, u + 1))
                        pe.wait_ge(diffT_copied.sem, diffT_copied.after(n, u))
                        for j in range(t + 1):
                            last = nc.tensor.transpose(trans[:, j * P:(j + 1) * P],
                                                       diff[:, h % 2, OFF[t] + j * P:OFF[t] + (j + 1) * P], ident[:, :])
                        last.then_inc(trans_done.sem, 1)
                    for n, u in units(b, stages, slot, LAG_PV):
                        h, t = divmod(u, NT)
                        if u == 0:
                            pe.wait_ge(v_copied.sem, v_copied.after(n, 1))
                        if t == 0:
                            pe.wait_ge(head_out.sem, head_out.after(n, h))
                        pe.wait_ge(diffT_copied.sem, diffT_copied.after(n, u + 1))
                        for j in range(t + 1):
                            last = nc.tensor.matmul(heads[:, t, :], diffT[:, u % 2, j * P:(j + 1) * P],
                                                    v_sb[:, j, h * HD:(h + 1) * HD], start=(j == 0), stop=(j == t))
                        last.then_inc(pv_done.sem, 1)

            run(pe, body)


def kernel(**inputs):
    import numpy as np
    import concourse.bacc as bacc
    from concourse.bass_utils import run_bass_kernel_spmd

    a = {k.removeprefix("L0_"): np.asarray(v) for k, v in inputs.items()}
    laid = {
        "x": a["attn_x"], "wqT": a["attn_Wq"].T, "wk1T": a["attn_Wk1"].T, "wk2T": a["attn_Wk2"].T,
        "wvT": a["attn_Wv"].T, "woT": a["attn_Wo"].T, "lam": a["attn_lambda_logit"].reshape(1, NH),
        "gamma": a["ffn_gamma"].reshape(D, 1), "beta": a["ffn_beta"].reshape(D, 1),
        "rwT": a["ffn_router_w"].T, "w1": a["ffn_W1"], "w2": a["ffn_W2"],
    }
    nc = bacc.Bacc("TRN2", target_bir_lowering=False, num_devices=1)
    arrays, args = {}, []
    for name, value in laid.items():
        arrays[f"{name}_dram"] = np.ascontiguousarray(value)
        args.append(nc.dram_tensor(f"{name}_dram", value.shape, FP32, kind="ExternalInput").ap())
    args.append(nc.dram_tensor("o_dram", (B, T, D), FP32, kind="ExternalOutput").ap())
    build(nc, *args)
    r = run_bass_kernel_spmd(nc, [arrays], core_ids=[0])
    return r.results[0]["o_dram"]
```

```python
import concourse.bass as bass
from concourse import mybir
from contextlib import ExitStack

FP32, BF16 = mybir.dt.float32, mybir.dt.bfloat16
ALU, ACT, AX = mybir.AluOpType, mybir.ActivationFunctionType, mybir.AxisListType

B, T, D = 8, 512, 128
NH, HD = 16, 8
P = 128
NT = T // P
E, F = 8, 512
NF = F // P
UNITS = NH * NT
QUAD = 4
QUADS = UNITS // QUAD
NG = NH // QUAD
STRIP = P // QUAD
SCALE = float(HD) ** -0.5
EPS, TEMP, DENOM_MIN = 1e-5, 1.5, 1e-6
MASKED = -1e30
CREDIT = 32

LAG_EXP = 1
LAG_DIFF = QUAD + LAG_EXP
LAG_TRANS = LAG_DIFF + 2
LAG_COPY = LAG_TRANS + 1
LAG_ABS = LAG_DIFF + 2
LAG_PV = LAG_TRANS + QUAD
LAG_SIDE = 1

SIDE = {}


def _place():
    def put(slot, *task):
        SIDE.setdefault(slot, []).append(task)

    put(8, "post", "spread")
    put(10, "post", "den_T")
    put(11, "post", "divide")
    put(13, "post", "out_proj")
    put(15, "post", "norm1")
    put(17, "post", "norm2")
    put(19, "post", "xn_T")
    put(20, "post", "logits")
    put(22, "post", "router_exp")
    put(22, "post", "route")
    slot = 21
    for e in range(E + 1):
        for n in range(NF):
            if e < E:
                put(slot, "post", "hidden", e, n)
                slot += 1
            if e:
                put(slot, "post", "expert", e - 1, n)
                slot += 1
    put(slot + 1, "post", "norm3")
    put(slot + 3, "post", "finish")
    for n, slot in enumerate((24, 29, 34, 39, 44)):
        put(slot, "prep", ("x_T", "proj", "proj", "proj", "values")[n], max(n - 1, 0))


_place()
POST_TASKS = [t for s in sorted(SIDE) for t in SIDE[s] if t[0] == "post"]
PREP_TASKS = [t for s in sorted(SIDE) for t in SIDE[s] if t[0] == "prep"]
PSUM_TASKS = ("den_T", "out_proj", "xn_T", "logits", "hidden", "expert", "x_T", "proj", "values")
STORED = (0, 1, 2, 0, 1)
PARTS_STORED = 3 + 2 * len(STORED)
WINDOWS = (0, 1, 2)
STACK = 3 * len(WINDOWS) * HD


class Signal:

    def __init__(self, sem, per_batch, step=1):
        self.sem, self.per, self.step = sem, per_batch, step

    def after(self, batch, n):
        value = (batch * self.per + n) * self.step + CREDIT
        return max(value, 1) if isinstance(value, int) else value


def build(nc, x, wqT, wk1T, wk2T, wvT, woT, lam, gamma, beta, rwT, w1, w2, out):
    ctx = ExitStack()
    with ctx:
        def sb(name, shape, dt=FP32):
            return ctx.enter_context(nc.sbuf_tensor(name, shape, dt))

        def pb(name, shape):
            return ctx.enter_context(nc.psum_tensor(name, shape, FP32))

        signals = []

        def signal(name, per_batch, step=1):
            signals.append(Signal(ctx.enter_context(nc.semaphore(name)), per_batch, step))
            return signals[-1]

        ident = sb("ident", [P, P])
        ident_bf = sb("ident_bf", [P, P], BF16)
        causal_bf = sb("causal_bf", [P, P], BF16)
        ones_row = sb("ones_row", [1, P])
        minus_half = sb("minus_half", [P, NT])
        eps_row = sb("eps_row", [P, NT])
        rank = sb("rank", [P, NT, E])
        lam_row = sb("lam_row", [1, NH])
        lam_all = sb("lam_all", [P, NH])
        gamma_col, beta_col = sb("gamma_col", [P, 1]), sb("beta_col", [P, 1])
        wq_sb = sb("wq_sb", [P, 3, P])
        wv_sb, wo_sb = sb("wv_sb", [P, P]), sb("wo_sb", [P, P])
        rw_sb = sb("rw_sb", [P, E])
        w1_sb = sb("w1_sb", [P, E, F])
        w2_sb = sb("w2_sb", [P, E, NF, D])

        x_in = sb("x_in", [P, NT, D])
        xT = sb("xT", [P, T])
        parts = sb("parts", [P, 3, 3, T], BF16)
        rest = sb("rest", [P, T])
        v_next = sb("v_next", [P, NT, D])
        v_sb = sb("v_sb", [P, NT, NH, STRIP])
        scratch = nc.dram_tensor("parts_dram", [3, NH, len(STORED), HD, T], BF16).ap()
        stack = sb("stack", [STACK, 3, NH, T], BF16)

        neg_max = sb("neg_max", [P, 2, QUAD, 2])
        sums = sb("sums", [P, 2, 2, QUAD])
        inv_l2 = sb("inv_l2", [P, QUAD])
        ratio = sb("ratio", [P, QUAD])
        coef = sb("coef", [P, 2, QUAD])
        floor = sb("floor", [P, 2, QUAD])
        exps = sb("exps", [P, 2, 2, QUAD, T])
        diff = exps[:, :, 1, :, :]
        diffT = sb("diffT", [P, 2, QUAD, T])
        abs_sum = sb("abs_sum", [P, QUAD])
        guard = sb("guard", [P, QUAD])
        inv_den = sb("inv_den", [P, NT, NH])
        inv_wide = sb("inv_wide", [P, NT, NH, HD])
        denT = sb("denT", [P, T])

        x_res = sb("x_res", [P, NT, D])
        attnT = sb("attnT", [P, T])
        r1 = sb("r1", [P, NT, D])
        x1 = sb("x1", [P, NT, D])
        xh = sb("xh", [P, NT, D])
        xnT = sb("xnT", [P, T])
        stats = sb("stats", [P, 3, NT, 6])
        mv = sb("mv", [P, 3, NT, 2])
        var_eps = sb("var_eps", [P, 3, NT])
        rstd = sb("rstd", [P, 3, NT])
        route_in = sb("route_in", [P, NT, E])
        route_max = sb("route_max", [P, NT])
        route_exp = sb("route_exp", [P, NT, E])
        route_inv = sb("route_inv", [P, NT])
        probs = sb("probs", [P, NT, E])
        top = sb("top", [P, 2, NT])
        first = sb("first", [P, 2, NT])
        hit = sb("hit", [P, 4, NT, E])
        gates = sb("gates", [P, NT, E])
        tanh_sb = sb("tanh_sb", [P, 2, T])
        hT = sb("hT", [P, 2, NF, T])
        x1_twice = sb("x1_twice", [P, NT, D])
        acc = sb("acc", [P, NT, D])
        y_out = sb("y_out", [P, NT, D])

        scores = pb("scores", [P, 2, 2, 512])
        trans = pb("trans", [P, NT * P])
        heads = pb("heads", [P, T])
        side = [pb(f"side{n}", [P, 512]) for n in range(2)]

        CONSTS = 9 + E
        weights_in = ctx.enter_context(nc.semaphore("weights_in"))
        consts_made = ctx.enter_context(nc.semaphore("consts_made"))
        lam_spread = ctx.enter_context(nc.semaphore("lam_spread"))
        lam_exp = ctx.enter_context(nc.semaphore("lam_exp"))
        lam_done = ctx.enter_context(nc.semaphore("lam_done"))
        x_loaded = signal("x_loaded", 1, 16)
        prep_psum = signal("prep_psum", len(PREP_TASKS))
        xT_copied = signal("xT_copied", 1)
        hi_made = signal("hi_made", 3)
        rest_made = signal("rest_made", 3)
        mid_made = signal("mid_made", 3)
        lo_made = signal("lo_made", 3)
        parts_out = signal("parts_out", PARTS_STORED, 16)
        stack_in = [signal(f"stack_in{g}", 3 * len(WINDOWS), 16) for g in range(NG)]
        v_evacuated = signal("v_evacuated", 1)
        v_copied = signal("v_copied", 1)
        score_done = signal("score_done", 2 * UNITS)
        max_done = signal("max_done", 2 * UNITS)
        exp_done = signal("exp_done", 2 * UNITS)
        coef_done = signal("coef_done", 3 * QUADS)
        scaled_done = signal("scaled_done", UNITS)
        diff_done = signal("diff_done", UNITS)
        abs_done = signal("abs_done", 2 * QUADS)
        trans_done = signal("trans_done", UNITS)
        diffT_copied = signal("diffT_copied", UNITS)
        pv_done = signal("pv_done", QUADS)
        den_done = signal("den_done", 2 * QUADS)
        res_loaded = signal("res_loaded", 1, 16)
        post_psum = signal("post_psum", 4)
        expert_psum = signal("expert_psum", E * (NF + NT))
        inv_spread = signal("inv_spread", 1)
        denT_copied = signal("denT_copied", 1)
        attnT_done = signal("attnT_done", 1)
        r1_done = signal("r1_done", 1)
        moments_done = signal("moments_done", 2)
        eps_added = signal("eps_added", 2)
        rstd_done = signal("rstd_done", 2)
        last_moments = signal("last_moments", 1)
        last_eps = signal("last_eps", 1)
        last_rstd = signal("last_rstd", 1)
        x1_done = signal("x1_done", 1)
        acc_set = signal("acc_set", 1)
        xh_done = signal("xh_done", 1)
        xnT_copied = signal("xnT_copied", 1)
        logit_step = signal("logit_step", 2)
        router_exp = signal("router_exp", 1)
        ROUTE_STEPS = 16
        route_step = signal("route_step", ROUTE_STEPS)
        tanh_done = signal("tanh_done", E * NF)
        hidden_done = signal("hidden_done", E * NF)
        expert_done = signal("expert_done", E * NT)
        y_done = signal("y_done", 1)
        y_stored = signal("y_stored", 1, 16)

        def reader(task):
            name = task[1]
            return {
                "den_T": (denT_copied, 1), "out_proj": (r1_done, 1), "xn_T": (xnT_copied, 1),
                "logits": (logit_step, 2), "x_T": (xT_copied, 1), "values": (v_evacuated, 1),
                "proj": (rest_made, task[2] + 1) if name == "proj" else None,
                "hidden": (hidden_done, NF * task[2] + task[3] + 1) if name == "hidden" else None,
                "expert": (expert_done, NT * task[2] + task[3] + 1) if name == "expert" else None,
            }[name]

        order = []
        for slot in range(UNITS):
            order += [("late", t) for t in SIDE.get(slot + UNITS, []) if t[1] in PSUM_TASKS]
            order += [(t[0], t) for t in SIDE.get(slot, []) if t[1] in PSUM_TASKS]
        bank_of = {t: n % 2 for n, (_, t) in enumerate(order)}
        psum_count = {}
        for tasks in (POST_TASKS, PREP_TASKS):
            for experts in (False, True):
                chosen = [t for t in tasks if t[1] in PSUM_TASKS and (t[1] in ("hidden", "expert")) == experts]
                for n, t in enumerate(chosen):
                    psum_count[t] = n + 1

        def psum_of(task):
            if task[1] in ("hidden", "expert"):
                return expert_psum
            return post_psum if task[0] == "post" else prep_psum

        def run(engine, body):
            body(-1, ("prep",))
            body(0, ("attention", "prep"))
            body(1, ("attention", "prep", "post"))
            with engine.Fori(2, B - 1) as b:
                body(b, ("attention", "prep", "post", "late"))
            body(B - 1, ("attention", "post", "late"))
            body(B, ("trail", "post", "late"))
            body(B + 1, ("late",))

        def units(b, stages, slot, lag):
            u = slot - lag
            if u >= 0:
                return [(b, u)] if "attention" in stages else []
            if "trail" in stages or ("attention" in stages and not (isinstance(b, int) and b == 0)):
                return [(b - 1, u + UNITS)]
            return []

        def side_tasks(b, stages, slot, lag=0):
            if "late" in stages:
                for task in SIDE.get(slot - lag + UNITS, []):
                    yield task, b - 2
            for task in SIDE.get(slot - lag, []):
                if task[0] in stages:
                    yield task, (b + 1 if task[0] == "prep" else b - 1)

        def tiles(ap):
            return ap.rearrange("p (t d) -> p t d", t=NT)

        block = ctx.enter_context(nc.Block())

        @block.sync
        def _(sp):
            for dst, src in ((wq_sb[:, 0, :], wqT), (wq_sb[:, 1, :], wk1T), (wq_sb[:, 2, :], wk2T),
                             (wv_sb[:, :], wvT), (wo_sb[:, :], woT), (rw_sb[:, :], rwT),
                             (gamma_col[:, :], gamma), (beta_col[:, :], beta), (lam_row[:, :], lam),
                             (w1_sb[:, :, :], w1.rearrange("e d f -> d e f")),
                             (w2_sb[:, :, :, :], w2.rearrange("e (n f) d -> f e n d", f=P))):
                sp.dma_start(dst, src).then_inc(weights_in, 16)
            for s in signals:
                sp.sem_inc(s.sem, CREDIT)

            def rows(ap, b):
                return ap[b, :, :].rearrange("(t p) d -> p t d", p=P) if isinstance(b, int) else \
                    ap[bass.ds(b, 1), :, :].rearrange("o (t p) d -> p (o t) d", p=P)

            def body(b, stages):
                if "prep" in stages:
                    n = b + 1
                    sp.wait_ge(prep_psum.sem, prep_psum.after(n - 1, 1))
                    sp.dma_start(x_in[:, :, :], rows(x, n)).then_inc(x_loaded.sem, 16)
                if "post" in stages:
                    sp.wait_ge(r1_done.sem, r1_done.after(b - 2, 1))
                    sp.dma_start(x_res[:, :, :], rows(x, b - 1)).then_inc(res_loaded.sem, 16)
                if "prep" in stages:
                    for z in range(3):
                        sp.wait_ge(lo_made.sem, lo_made.after(n, z + 1))
                        for g in range(NG):
                            sp.wait_ge(stack_in[g].sem, stack_in[g].after(n - 1, 3 * len(WINDOWS)))
                        for slot, part in enumerate(STORED if z else STORED[:3]):
                            sp.dma_start(scratch[z, :, slot, :, :], parts[:, z, part, :]).then_inc(parts_out.sem, 16)
                    sp.wait_ge(parts_out.sem, parts_out.after(n, PARTS_STORED))
                    for g in range(NG):
                        hs = slice(g * QUAD, (g + 1) * QUAD)
                        sp.wait_ge(score_done.sem, score_done.after(n - 1, 2 * (g + 1) * QUAD * NT))

                        def stored(z, slot):
                            return scratch[z, g:NH:NG, slot:slot + 3, :, :].rearrange("h s d t -> (s d) h t")

                        for z in range(3):
                            for i, window in enumerate(WINDOWS):
                                sp.dma_start(stack[3 * HD * i:3 * HD * (i + 1), z, hs, :], stored(z, window if z else 0))\
                                  .then_inc(stack_in[g].sem, 16)
                if "late" in stages:
                    sp.wait_ge(y_done.sem, y_done.after(b - 2, 1))
                    sp.dma_start(rows(out, b - 2), y_out[:, :, :]).then_inc(y_stored.sem, 16)

            run(sp, body)
            sp.wait_ge(y_stored.sem, y_stored.after(B - 1, 1))
            sp.wait_ge(parts_out.sem, parts_out.after(B - 1, PARTS_STORED))

        @block.gpsimd
        def _(pool):
            nc.gpsimd.memset(ident[:, :], 0.0).then_inc(consts_made, 1)
            nc.gpsimd.memset(causal_bf[:, :], 0.0).then_inc(consts_made, 1)
            nc.gpsimd.memset(ones_row[:, :], 1.0).then_inc(consts_made, 1)
            nc.gpsimd.memset(minus_half[:, :], -0.5).then_inc(consts_made, 1)
            nc.gpsimd.memset(eps_row[:, :], EPS).then_inc(consts_made, 1)
            for e in range(E):
                nc.gpsimd.memset(rank[:, :, e:e + 1], float(E - e)).then_inc(consts_made, 1)
            nc.gpsimd.memset(v_sb[:, :, :, :], 0.0).then_inc(consts_made, 1)
            pool.wait_ge(consts_made, CONSTS - 3)
            nc.gpsimd.affine_select(out=ident[:, :], in_=ident[:, :], compare_op=ALU.not_equal, fill=1.0,
                                    base=0, pattern=[[-1, P]], channel_multiplier=1).then_inc(consts_made, 1)
            nc.gpsimd.affine_select(out=causal_bf[:, :], in_=causal_bf[:, :], compare_op=ALU.is_ge, fill=MASKED,
                                    base=0, pattern=[[-1, P]], channel_multiplier=1).then_inc(consts_made, 1)
            pool.wait_ge(consts_made, CONSTS - 1)
            nc.gpsimd.tensor_copy(ident_bf[:, :], ident[:, :]).then_inc(consts_made, 1)

            def body(b, stages):
                for slot in range(UNITS):
                    for n, u in units(b, stages, slot, LAG_DIFF):
                        q, j = divmod(u, QUAD)
                        w = (q % NT + 1) * P
                        pool.wait_ge(coef_done.sem, coef_done.after(n, 3 * (q + 1)))
                        nc.gpsimd.tensor_tensor(diff[:, q % 2, j, 0:w], exps[:, q % 2, 1, j, 0:w],
                                                coef[:, q % 2, j:j + 1].broadcast_to([P, w]), ALU.mult)\
                            .then_inc(scaled_done.sem, 1)
                        pool.wait_ge(scaled_done.sem, scaled_done.after(n, u + 1))
                        nc.gpsimd.tensor_tensor(diff[:, q % 2, j, 0:w], diff[:, q % 2, j, 0:w],
                                                exps[:, q % 2, 0, j, 0:w], ALU.subtract).then_inc(diff_done.sem, 1)
                    for task, n in side_tasks(b, stages, slot, 2 * LAG_SIDE):
                        name = task[1]
                        if name == "proj":
                            z = task[2]
                            pool.wait_ge(mid_made.sem, mid_made.after(n, z + 1))
                            nc.gpsimd.tensor_tensor(parts[:, z, 2, :], rest[:, :], parts[:, z, 1, :],
                                                    ALU.subtract).then_inc(lo_made.sem, 1)
                        if name in ("out_proj", "norm1", "norm3"):
                            i = ("out_proj", "norm1", "norm3").index(name)
                            moments, added, done = (moments_done, eps_added, rstd_done) if i < 2 else \
                                (last_moments, last_eps, last_rstd)
                            k = i + 1 if i < 2 else 1
                            pool.wait_ge(moments.sem, moments.after(n, k))
                            nc.gpsimd.tensor_tensor(var_eps[:, i, :], mv[:, i, :, 1], eps_row[:, :], ALU.add)\
                                .then_inc(added.sem, 1)
                            pool.wait_ge(added.sem, added.after(n, k))
                            nc.gpsimd.tensor_tensor(rstd[:, i, :], var_eps[:, i, :], minus_half[:, :], ALU.pow)\
                                .then_inc(done.sem, 1)

            run(pool, body)

        @block.scalar
        def _(act):
            act.wait_ge(lam_spread, 1)
            nc.scalar.activation(lam_all[:, :], side[0][:, 0:NH], ACT.Exp, scale=-1.0).then_inc(lam_exp, 1)

            def body(b, stages):
                for slot in range(UNITS):
                    for k in range(2):
                        for n, u in units(b, stages, slot, LAG_EXP):
                            q, j = divmod(u, QUAD)
                            w = (q % NT + 1) * P
                            if k == 0:
                                act.wait_ge(diff_done.sem, diff_done.after(n, u + 1 - 2 * QUAD))
                            else:
                                act.wait_ge(trans_done.sem, trans_done.after(n, u + 1 - 2 * QUAD))
                                act.wait_ge(abs_done.sem, abs_done.after(n, 2 * (q - 2) + j // 2 + 1))
                            act.wait_ge(max_done.sem, max_done.after(n, 2 * u + k + 1))
                            nc.scalar.activation(exps[:, q % 2, k, j, 0:w], scores[:, u % 2, k, 0:w],
                                                 ACT.Exp, bias=neg_max[:, q % 2, j, k:k + 1],
                                                 accum_out=sums[:, q % 2, k, j:j + 1]).then_inc(exp_done.sem, 1)
                        for n, u in units(b, stages, slot, LAG_COPY) if k == 0 else ():
                            q, j = divmod(u, QUAD)
                            w = (q % NT + 1) * P
                            act.wait_ge(trans_done.sem, trans_done.after(n, u + 1))
                            act.wait_ge(pv_done.sem, pv_done.after(n, q - 1))
                            nc.scalar.activation(diffT[:, q % 2, j, 0:w], trans[:, 0:w], ACT.Copy)\
                                .then_inc(diffT_copied.sem, 1)
                    for task, n in side_tasks(b, stages, slot):
                        name = task[1]
                        bank = side[bank_of[task]] if task in bank_of else None
                        if name == "x_T":
                            act.wait_ge(psum_of(task).sem, psum_of(task).after(n, psum_count[task]))
                            act.wait_ge(prep_psum.sem, prep_psum.after(n - 1, len(PREP_TASKS)))
                            nc.scalar.activation(xT[:, :], bank[:, :], ACT.Copy).then_inc(xT_copied.sem, 1)
                        if name == "proj":
                            z = task[2]
                            act.wait_ge(psum_of(task).sem, psum_of(task).after(n, psum_count[task]))
                            act.wait_ge(parts_out.sem, parts_out.after(n - 1, PARTS_STORED))
                            nc.scalar.activation(parts[:, z, 0, :], bank[:, :], ACT.Copy,
                                                 scale=SCALE if z == 0 else 1.0).then_inc(hi_made.sem, 1)
                        if name == "values":
                            act.wait_ge(psum_of(task).sem, psum_of(task).after(n, psum_count[task]))
                            act.wait_ge(v_copied.sem, v_copied.after(n - 1, 1))
                            nc.scalar.activation(v_next[:, :, :], tiles(bank[:, :]), ACT.Copy)\
                                .then_inc(v_evacuated.sem, 1)
                        if name == "den_T":
                            act.wait_ge(psum_of(task).sem, psum_of(task).after(n, psum_count[task]))
                            nc.scalar.activation(denT[:, :], bank[:, :], ACT.Copy).then_inc(denT_copied.sem, 1)
                        if name == "xn_T":
                            act.wait_ge(psum_of(task).sem, psum_of(task).after(n, psum_count[task]))
                            act.wait_ge(expert_psum.sem, expert_psum.after(n - 1, psum_count[("post", "hidden", E - 1, NF - 1)]))
                            nc.scalar.activation(xnT[:, :], bank[:, :], ACT.Identity, bias=beta_col[:, 0:1],
                                                 scale=gamma_col[:, 0:1]).then_inc(xnT_copied.sem, 1)
                        if name == "router_exp":
                            act.wait_ge(logit_step.sem, logit_step.after(n, 2))
                            act.wait_ge(route_step.sem, route_step.after(n - 1, ROUTE_STEPS))
                            nc.scalar.activation(route_exp[:, :, :], route_in[:, :, :], ACT.Exp, scale=1.0 / TEMP)\
                                .then_inc(router_exp.sem, 1)
                        if name == "hidden":
                            i = NF * task[2] + task[3]
                            act.wait_ge(psum_of(task).sem, psum_of(task).after(n, psum_count[task]))
                            act.wait_ge(hidden_done.sem, hidden_done.after(n, i - 1))
                            nc.scalar.activation(tanh_sb[:, i % 2, :], bank[:, :], ACT.Tanh, scale=0.5)\
                                .then_inc(tanh_done.sem, 1)

            run(act, body)

        @block.vector
        def _(dve):
            dve.wait_ge(lam_exp, 1)
            nc.vector.tensor_scalar_add(lam_all[:, :], lam_all[:, :], 1.0).then_inc(lam_done, 1)
            dve.wait_ge(lam_done, 1)
            nc.vector.reciprocal(lam_all[:, :], lam_all[:, :]).then_inc(lam_done, 1)
            dve.wait_ge(lam_done, 2)
            dve.wait_ge(consts_made, CONSTS)

            def moments(n, i, src):
                for t in range(NT):
                    nc.vector.bn_stats(stats[:, i, t, :], src[:, t, :])
                nc.vector.drain()
                for t in range(NT):
                    last = nc.vector.bn_aggr(mv[:, i, t, :], stats[:, i, t, :])
                last.then_inc((moments_done if i < 2 else last_moments).sem, 1)

            def normalise(n, i, dst, src):
                if i < 2:
                    dve.wait_ge(rstd_done.sem, rstd_done.after(n, i + 1))
                else:
                    dve.wait_ge(last_rstd.sem, last_rstd.after(n, 1))
                for t in range(NT):
                    last = nc.vector.tensor_scalar(dst[:, t, :], src[:, t, :], mv[:, i, t, 0:1],
                                                   rstd[:, i, t:t + 1], ALU.subtract, ALU.mult)
                return last

            def route(n):
                count = [0]

                def step(instruction):
                    count[0] += 1
                    instruction.then_inc(route_step.sem, 1)
                    dve.wait_ge(route_step.sem, route_step.after(n, count[0]))

                def over_experts(a):
                    return a.unsqueeze(2).broadcast_to([P, NT, E])

                dve.wait_ge(router_exp.sem, router_exp.after(n, 1))
                step(nc.vector.tensor_reduce(route_inv[:, :], route_exp[:, :, :], AX.X, ALU.add))
                step(nc.vector.reciprocal(route_inv[:, :], route_inv[:, :]))
                step(nc.vector.tensor_tensor(probs[:, :, :], route_exp[:, :, :], over_experts(route_inv[:, :]), ALU.mult))
                for k in range(2):
                    left = probs if k == 0 else hit[:, 3, :, :]
                    left = left[:, :, :]
                    step(nc.vector.tensor_reduce(top[:, k, :], left, AX.X, ALU.max))
                    step(nc.vector.tensor_tensor(hit[:, 2, :, :], left, over_experts(top[:, k, :]), ALU.is_equal))
                    step(nc.vector.tensor_tensor(hit[:, 2, :, :], hit[:, 2, :, :], rank[:, :, :], ALU.mult))
                    step(nc.vector.tensor_reduce(first[:, k, :], hit[:, 2, :, :], AX.X, ALU.max))
                    step(nc.vector.tensor_tensor(hit[:, k, :, :], rank[:, :, :], over_experts(first[:, k, :]), ALU.is_equal))
                    if k == 0:
                        step(nc.vector.scalar_tensor_tensor(out=hit[:, 3, :, :], in0=hit[:, 0, :, :], scalar=-2.0,
                                                            in1=probs[:, :, :], op0=ALU.mult, op1=ALU.add))
                return count

            def body(b, stages):
                for slot in range(UNITS):
                    for task, n in side_tasks(b, stages, slot, LAG_SIDE):
                        name = task[1]
                        bank = side[bank_of[task]] if task in bank_of else None
                        if name == "proj":
                            z = task[2]
                            dve.wait_ge(psum_of(task).sem, psum_of(task).after(n, psum_count[task]))
                            dve.wait_ge(hi_made.sem, hi_made.after(n, z + 1))
                            dve.wait_ge(lo_made.sem, lo_made.after(n, z))
                            nc.vector.scalar_tensor_tensor(out=rest[:, :], in0=bank[:, :],
                                                           scalar=SCALE if z == 0 else 1.0, in1=parts[:, z, 0, :],
                                                           op0=ALU.mult, op1=ALU.subtract).then_inc(rest_made.sem, 1)
                            dve.wait_ge(rest_made.sem, rest_made.after(n, z + 1))
                            nc.vector.tensor_copy(parts[:, z, 1, :], rest[:, :]).then_inc(mid_made.sem, 1)
                        if name == "spread":
                            dve.wait_ge(den_done.sem, den_done.after(n, 2 * QUADS))
                            dve.wait_ge(post_psum.sem, post_psum.after(n - 1, psum_count[("post", "den_T")]))
                            nc.vector.tensor_copy(inv_wide[:, :, :, :],
                                                  inv_den[:, :, :].unsqueeze(3).broadcast_to([P, NT, NH, HD]))\
                                .then_inc(inv_spread.sem, 1)
                        if name == "divide":
                            dve.wait_ge(denT_copied.sem, denT_copied.after(n, 1))
                            dve.wait_ge(pv_done.sem, pv_done.after(n, QUADS))
                            nc.vector.scalar_tensor_tensor(out=attnT[:, :], in0=heads[:, :], scalar=-1.0,
                                                           in1=denT[:, :], op0=ALU.mult, op1=ALU.mult)\
                                .then_inc(attnT_done.sem, 1)
                        if name == "out_proj":
                            dve.wait_ge(psum_of(task).sem, psum_of(task).after(n, psum_count[task]))
                            dve.wait_ge(res_loaded.sem, res_loaded.after(n, 1))
                            nc.vector.tensor_tensor(r1[:, :, :], tiles(bank[:, :]), x_res[:, :, :], ALU.add)\
                                .then_inc(r1_done.sem, 1)
                            dve.wait_ge(r1_done.sem, r1_done.after(n, 1))
                            moments(n, 0, r1)
                        if name == "norm1":
                            normalise(n, 0, x1, r1).then_inc(x1_done.sem, 1)
                            dve.wait_ge(x1_done.sem, x1_done.after(n, 1))
                            moments(n, 1, x1)
                        if name == "norm2":
                            nc.vector.tensor_scalar(x1_twice[:, :, :], x1[:, :, :], 2.0, None, ALU.mult)\
                                .then_inc(acc_set.sem, 1)
                            normalise(n, 1, xh, x1).then_inc(xh_done.sem, 1)
                        if name == "logits":
                            dve.wait_ge(psum_of(task).sem, psum_of(task).after(n, psum_count[task]))
                            logits = bank[:, 0:NT * E].rearrange("p (t e) -> p t e", t=NT)
                            nc.vector.tensor_reduce(route_max[:, :], logits, AX.X, ALU.max)\
                                .then_inc(logit_step.sem, 1)
                            dve.wait_ge(logit_step.sem, logit_step.after(n, 1))
                            nc.vector.tensor_tensor(route_in[:, :, :], logits,
                                                    route_max[:, :].unsqueeze(2).broadcast_to([P, NT, E]),
                                                    ALU.subtract).then_inc(logit_step.sem, 1)
                        if name == "route":
                            count = route(n)

                            def step(instruction):
                                count[0] += 1
                                instruction.then_inc(route_step.sem, 1)
                                dve.wait_ge(route_step.sem, route_step.after(n, count[0]))
                            step(nc.vector.tensor_tensor(hit[:, 2, :, :], hit[:, 0, :, :], hit[:, 1, :, :], ALU.add))
                            nc.vector.scalar_tensor_tensor(out=gates[:, :, :], in0=hit[:, 2, :, :], scalar=0.5,
                                                           in1=probs[:, :, :], op0=ALU.mult, op1=ALU.mult)\
                                .then_inc(route_step.sem, 1)
                            count[0] += 1
                            pass
                            route_total.append(count[0])
                        if name == "hidden":
                            e, f = task[2], task[3]
                            i = NF * e + f
                            dve.wait_ge(tanh_done.sem, tanh_done.after(n, i + 1))
                            m, used = (n, e - 2) if e >= 2 else (n - 1, e + E - 2)
                            used = ("post", "expert", used, NT - 1)
                            dve.wait_ge(expert_psum.sem, expert_psum.after(m, psum_count[used]))
                            nc.vector.scalar_tensor_tensor(out=hT[:, e % 2, f, :], in0=tanh_sb[:, i % 2, :],
                                                           scalar=1.0, in1=bank[:, :], op0=ALU.add, op1=ALU.mult)\
                                .then_inc(hidden_done.sem, 1)
                        if name == "expert":
                            e, t = task[2], task[3]
                            dve.wait_ge(psum_of(task).sem, psum_of(task).after(n, psum_count[task]))
                            if e == 0:
                                dve.wait_ge(route_step.sem, route_step.after(n, ROUTE_STEPS))
                                dve.wait_ge(acc_set.sem, acc_set.after(n, 1))
                            else:
                                dve.wait_ge(expert_done.sem, expert_done.after(n, NT * (e - 1) + t + 1))
                            nc.vector.scalar_tensor_tensor(
                                out=acc[:, t, :], in0=bank[:, 0:D], scalar=gates[:, t, e:e + 1],
                                in1=(acc if e else x1_twice)[:, t, :], op0=ALU.mult, op1=ALU.add).then_inc(expert_done.sem, 1)
                        if name == "norm3":
                            dve.wait_ge(expert_done.sem, expert_done.after(n, NT * E))
                            moments(n, 2, acc)
                        if name == "finish":
                            dve.wait_ge(y_stored.sem, y_stored.after(n - 1, 1))
                            normalise(n, 2, y_out, acc).then_inc(y_done.sem, 1)
                    for n, u in units(b, stages, slot, 0):
                        q, j = divmod(u, QUAD)
                        w = (q % NT + 1) * P
                        dve.wait_ge(exp_done.sem, exp_done.after(n, 2 * (u + 1 - 2 * QUAD)))
                        for k in range(2):
                            dve.wait_ge(score_done.sem, score_done.after(n, 2 * u + k + 1))
                            nc.vector.tensor_reduce(neg_max[:, q % 2, j, k:k + 1], scores[:, u % 2, k, 0:w], AX.X,
                                                    ALU.max, negate=True).then_inc(max_done.sem, 1)
                    for n, u in units(b, stages, slot, LAG_DIFF):
                        q, j = divmod(u, QUAD)
                        if j:
                            continue
                        dve.wait_ge(exp_done.sem, exp_done.after(n, 2 * (u + QUAD)))
                        dve.wait_ge(diff_done.sem, diff_done.after(n, u - QUAD))
                        nc.vector.reciprocal(inv_l2[:, :], sums[:, q % 2, 1, :]).then_inc(coef_done.sem, 1)
                        nc.vector.tensor_scalar(floor[:, q % 2, :], sums[:, q % 2, 0, :], DENOM_MIN, None, ALU.mult)
                        dve.wait_ge(coef_done.sem, coef_done.after(n, 3 * q + 1))
                        nc.vector.tensor_tensor(ratio[:, :], sums[:, q % 2, 0, :], inv_l2[:, :], ALU.mult)\
                            .then_inc(coef_done.sem, 1)
                        dve.wait_ge(coef_done.sem, coef_done.after(n, 3 * q + 2))
                        nc.vector.tensor_tensor(coef[:, q % 2, :], ratio[:, :], lam_all[:, q // NT:NH:NG], ALU.mult)\
                            .then_inc(coef_done.sem, 1)
                    for n, u in units(b, stages, slot, LAG_ABS):
                        q, j = divmod(u, QUAD)
                        if j % 2 == 0:
                            continue
                        w = (q % NT + 1) * P
                        dve.wait_ge(diff_done.sem, diff_done.after(n, u + 1))
                        nc.vector.tensor_reduce(abs_sum[:, j - 1:j + 1], diff[:, q % 2, j - 1:j + 1, 0:w], AX.X,
                                                ALU.add, apply_absolute_value=True).then_inc(abs_done.sem, 1)
                        if j < QUAD - 1:
                            continue
                        dve.wait_ge(abs_done.sem, abs_done.after(n, 2 * (q + 1)))
                        nc.vector.tensor_tensor(guard[:, :], abs_sum[:, :], floor[:, q % 2, :], ALU.max)\
                            .then_inc(den_done.sem, 1)
                        dve.wait_ge(den_done.sem, den_done.after(n, 2 * q + 1))
                        nc.vector.reciprocal(inv_den[:, q % NT, q // NT:NH:NG], guard[:, :]).then_inc(den_done.sem, 1)
                    if slot == LAG_PV and "attention" in stages:
                        dve.wait_ge(v_evacuated.sem, v_evacuated.after(b, 1))
                        dve.wait_ge(pv_done.sem, pv_done.after(b - 1, QUADS))
                        for g in range(NG):
                            last = nc.vector.tensor_copy(
                                v_sb[:, :, g:NH:NG, g * HD:(g + 1) * HD],
                                v_next[:, :, :].rearrange("p t (h d) -> p t h d", d=HD)[:, :, g:NH:NG, :])
                        last.then_inc(v_copied.sem, 1)

            route_total = []
            run(dve, body)
            assert set(route_total) == {ROUTE_STEPS}, route_total

        @block.tensor
        def _(pe):
            pe.wait_ge(weights_in, 11 * 16)
            pe.wait_ge(consts_made, CONSTS)
            nc.tensor.matmul(side[0][:, 0:NH], ones_row[:, :], lam_row[:, :], start=True, stop=True)\
                .then_inc(lam_spread, 1)
            pe.wait_ge(lam_done, 2)

            def side_task(task, n, waits):
                name = task[1]
                bank = side[bank_of[task]]
                for s, m, k in waits:
                    pe.wait_ge(s.sem, s.after(m, k))
                col = slice(0, P)
                if name == "x_T":
                    pe.wait_ge(x_loaded.sem, x_loaded.after(n, 1))
                    for t in range(NT):
                        last = nc.tensor.transpose(bank[:, t * P:(t + 1) * P], x_in[:, t, :], ident[:, :])
                if name == "proj":
                    pe.wait_ge(xT_copied.sem, xT_copied.after(n, 1))
                    last = nc.tensor.matmul(bank[:, :], wq_sb[:, task[2], :], xT[:, :], start=True, stop=True)
                if name == "values":
                    pe.wait_ge(xT_copied.sem, xT_copied.after(n, 1))
                    for t in range(NT):
                        last = nc.tensor.matmul(bank[:, t * P:(t + 1) * P], xT[:, t * P:(t + 1) * P], wv_sb[:, :],
                                                start=True, stop=True)
                if name == "den_T":
                    pe.wait_ge(inv_spread.sem, inv_spread.after(n, 1))
                    for t in range(NT):
                        last = nc.tensor.transpose(bank[:, t * P:(t + 1) * P],
                                                   inv_wide[:, t, :, :].rearrange("p h d -> p (h d)"), ident[:, :])
                if name == "out_proj":
                    pe.wait_ge(attnT_done.sem, attnT_done.after(n, 1))
                    for t in range(NT):
                        last = nc.tensor.matmul(bank[:, t * P:(t + 1) * P], attnT[:, t * P:(t + 1) * P], wo_sb[:, :],
                                                start=True, stop=True)
                if name == "xn_T":
                    pe.wait_ge(xh_done.sem, xh_done.after(n, 1))
                    for t in range(NT):
                        last = nc.tensor.transpose(bank[:, t * P:(t + 1) * P], xh[:, t, :], ident[:, :])
                if name == "logits":
                    pe.wait_ge(xnT_copied.sem, xnT_copied.after(n, 1))
                    for t in range(NT):
                        last = nc.tensor.matmul(bank[:, t * E:(t + 1) * E], xnT[:, t * P:(t + 1) * P], rw_sb[:, :],
                                                start=True, stop=True)
                if name == "hidden":
                    e, f = task[2], task[3]
                    pe.wait_ge(xnT_copied.sem, xnT_copied.after(n, 1))
                    last = nc.tensor.matmul(bank[:, :], w1_sb[:, e, f * P:(f + 1) * P], xnT[:, :],
                                            start=True, stop=True)
                if name == "expert":
                    e, t = task[2], task[3]
                    pe.wait_ge(hidden_done.sem, hidden_done.after(n, NF * (e + 1)))
                    for f in range(NF):
                        last = nc.tensor.matmul(bank[:, 0:D], hT[:, e % 2, f, t * P:(t + 1) * P],
                                                w2_sb[:, e, f, :], start=(f == 0), stop=(f == NF - 1))
                last.then_inc(psum_of(task).sem, 1)

            def bank_waits(b, stages):
                batch = {"prep": b + 1, "post": b - 1, "late": b - 2}
                last = [{}, {}]
                for kind, t in order:
                    last[bank_of[t]][kind] = (t, batch[kind] - 1)
                found = {}
                for kind, t in order:
                    if kind not in stages:
                        continue
                    waits = []
                    for p, m in last[bank_of[t]].values():
                        m = min(m, B - 1) if isinstance(m, int) else m
                        if not (isinstance(m, int) and m < 0):
                            waits.append((*reader(p)[:1], m, reader(p)[1]))
                    found[t] = waits
                    last[bank_of[t]] = {kind: (t, batch[kind])}
                return found

            def body(b, stages):
                waits = bank_waits(b, stages)
                for slot in range(UNITS):
                    for n, u in units(b, stages, slot, 0):
                        q, j = divmod(u, QUAD)
                        g, t = divmod(q, NT)
                        w = (t + 1) * P
                        if t == 0 and j == 0:
                            pe.wait_ge(stack_in[g].sem, stack_in[g].after(n, 3 * len(WINDOWS)))
                        for k in range(2):
                            pe.wait_ge(exp_done.sem, exp_done.after(n, 2 * (u - 2) + k + 1))
                            nc.tensor.matmul(scores[:, u % 2, k, 0:w], stack[:, 0, QUAD * g + j, t * P:(t + 1) * P],
                                             stack[:, 1 + k, QUAD * g + j, 0:w], start=True, stop=False)
                            nc.tensor.matmul(scores[:, u % 2, k, w - P:w], ident_bf[:, :], causal_bf[:, :],
                                             start=False, stop=True).then_inc(score_done.sem, 1)
                    for task, n in side_tasks(b, stages, slot):
                        if task in bank_of:
                            side_task(task, n, waits[task])
                    for n, u in units(b, stages, slot, LAG_TRANS):
                        q, j = divmod(u, QUAD)
                        pe.wait_ge(diff_done.sem, diff_done.after(n, u + 1))
                        pe.wait_ge(diffT_copied.sem, diffT_copied.after(n, u))
                        for i in range(q % NT + 1):
                            last = nc.tensor.transpose(trans[:, i * P:(i + 1) * P],
                                                       diff[:, q % 2, j, i * P:(i + 1) * P], ident[:, :])
                        last.then_inc(trans_done.sem, 1)
                    for n, u in units(b, stages, slot, LAG_PV):
                        q, j = divmod(u, QUAD)
                        g, t = divmod(q, NT)
                        i = j - (QUAD - 1 - t)
                        if i < 0:
                            continue
                        if q == 0:
                            pe.wait_ge(v_copied.sem, v_copied.after(n, 1))
                            pe.wait_ge(attnT_done.sem, attnT_done.after(n - 1, 1))
                        pe.wait_ge(diffT_copied.sem, diffT_copied.after(n, QUAD * (q + 1)))
                        for k in range(QUAD):
                            last = nc.tensor.matmul(
                                heads[k * STRIP:(k + 1) * STRIP, t * P:(t + 1) * P], v_sb[:, i, NG * k + g, :],
                                diffT[:, q % 2, k, i * P:(i + 1) * P],
                                start=(q == 0 and i == 0), stop=(g == NG - 1 and i == t), skip_group_check=True)
                        if i == t:
                            last.then_inc(pv_done.sem, 1)

            run(pe, body)


def kernel(**inputs):
    import numpy as np
    import concourse.bacc as bacc
    from concourse.bass_utils import run_bass_kernel_spmd

    a = {k.removeprefix("L0_"): np.asarray(v) for k, v in inputs.items()}
    laid = {
        "x": a["attn_x"], "wqT": a["attn_Wq"].T, "wk1T": a["attn_Wk1"].T, "wk2T": a["attn_Wk2"].T,
        "wvT": a["attn_Wv"].T, "woT": a["attn_Wo"].T, "lam": a["attn_lambda_logit"].reshape(1, NH),
        "gamma": a["ffn_gamma"].reshape(D, 1), "beta": a["ffn_beta"].reshape(D, 1),
        "rwT": a["ffn_router_w"].T, "w1": a["ffn_W1"], "w2": a["ffn_W2"],
    }
    nc = bacc.Bacc("TRN2", target_bir_lowering=False, num_devices=1)
    arrays, args = {}, []
    for name, value in laid.items():
        arrays[f"{name}_dram"] = np.ascontiguousarray(value)
        args.append(nc.dram_tensor(f"{name}_dram", value.shape, FP32, kind="ExternalInput").ap())
    args.append(nc.dram_tensor("o_dram", (B, T, D), FP32, kind="ExternalOutput").ap())
    build(nc, *args)
    r = run_bass_kernel_spmd(nc, [arrays], core_ids=[0])
    return r.results[0]["o_dram"]
```

```python
import concourse.bass as bass
from concourse import mybir
from contextlib import ExitStack

FP32, BF16 = mybir.dt.float32, mybir.dt.bfloat16
ALU, ACT, AX = mybir.AluOpType, mybir.ActivationFunctionType, mybir.AxisListType

B, T, D = 8, 512, 128
NH, HD = 16, 8
P = 128
NT = T // P
E, F = 8, 512
NF = F // P
UNITS = NH * NT
QUAD = 4
QUADS = UNITS // QUAD
NG = NH // QUAD
TILE_ORDER = (1, 0, 2, 3)
STRIP = P // QUAD
SCALE = float(HD) ** -0.5
EPS, TEMP, DENOM_MIN = 1e-5, 1.5, 1e-6
MASKED = -1e30
CREDIT = 32

LAG_EXP = 1
LAG_DIFF = QUAD + LAG_EXP
LAG_TRANS = LAG_DIFF + 2
LAG_COPY = LAG_TRANS + 1
LAG_ABS = LAG_DIFF + 2
LAG_DEN = LAG_ABS + 2
LAG_PV = LAG_COPY + QUAD
LAG_SIDE = 1

SIDE = {}
POST_SLOTS = {"spread": 8, "den_T": 9, "divide": 11, "out_proj": 13, "norm1": 15, "norm2": 18,
              "xn_T": 19, "logits": 21, "router_exp": 22}
FIRST_EXPERT_SLOT = 20
EXPERT_TASKS = (1, 2, 1, 1, 1, 1, 1, 1, 0, 1, 1, 1, 1, 1, 1, 1)
PREP_SLOTS = (24, 29, 36, 42, 43)


def tile_of(q):
    return TILE_ORDER[q % NT]


def _place():
    def put(slot, *task):
        SIDE.setdefault(slot, []).append(task)

    for name, slot in POST_SLOTS.items():
        put(slot, "post", name)
    tasks = []
    for e in range(E + 1):
        for n in range(NF):
            if e < E:
                tasks.append(("post", "hidden", e, n))
            if e:
                tasks.append(("post", "expert", e - 1, n))
    slot = FIRST_EXPERT_SLOT
    while tasks:
        for _ in range(min(EXPERT_TASKS[slot % len(EXPERT_TASKS)], len(tasks))):
            put(slot, *tasks.pop(0))
        slot += 1
    put(slot + 1, "post", "norm3")
    put(slot + 3, "post", "finish")
    for n, slot in enumerate(PREP_SLOTS):
        put(slot, "prep", ("x_T", "proj", "proj", "proj", "values")[n], max(n - 1, 0))


_place()
ROUTE_STEPS, ROUTE_PLACES = 16, 4
ROUTE_SLOT = next(slot for slot in SIDE for t in SIDE[slot] if t[1] == "router_exp") + 1
POST_TASKS = [t for s in sorted(SIDE) for t in SIDE[s] if t[0] == "post"]
PREP_TASKS = [t for s in sorted(SIDE) for t in SIDE[s] if t[0] == "prep"]
PSUM_TASKS = ("den_T", "out_proj", "xn_T", "logits", "hidden", "expert", "x_T", "proj", "values")
STORED = (0, 1, 2, 0, 1)
PARTS_STORED = (3, len(STORED), len(STORED))
WINDOWS = (0, 1, 2)
STACK = 3 * len(WINDOWS) * HD


class Signal:

    def __init__(self, sem, per_batch, step=1):
        self.sem, self.per, self.step = sem, per_batch, step

    def after(self, batch, n):
        value = (batch * self.per + n) * self.step + CREDIT
        return max(value, 1) if isinstance(value, int) else value


def build(nc, x, wqT, wk1T, wk2T, wvT, woT, lam, gamma, beta, rwT, w1, w2, out):
    ctx = ExitStack()
    with ctx:
        def sb(name, shape, dt=FP32):
            return ctx.enter_context(nc.sbuf_tensor(name, shape, dt))

        def pb(name, shape):
            return ctx.enter_context(nc.psum_tensor(name, shape, FP32))

        signals = []

        def signal(name, per_batch, step=1):
            signals.append(Signal(ctx.enter_context(nc.semaphore(name)), per_batch, step))
            return signals[-1]

        ident = sb("ident", [P, P])
        ident_bf = sb("ident_bf", [P, P], BF16)
        causal_bf = sb("causal_bf", [P, P], BF16)
        ones_row = sb("ones_row", [1, P])
        minus_half = sb("minus_half", [P, NT])
        eps_row = sb("eps_row", [P, NT])
        rank = sb("rank", [P, NT, E])
        lam_row = sb("lam_row", [1, NH])
        lam_all = sb("lam_all", [P, NH])
        gamma_col, beta_col = sb("gamma_col", [P, 1]), sb("beta_col", [P, 1])
        wq_sb = sb("wq_sb", [P, 3, P])
        wv_sb, wo_sb = sb("wv_sb", [P, P]), sb("wo_sb", [P, P])
        rw_sb = sb("rw_sb", [P, E])
        w1_sb = sb("w1_sb", [P, E, F])
        w2_sb = sb("w2_sb", [P, E, NF, D])

        x_in = sb("x_in", [P, NT, D])
        xT = sb("xT", [P, T])
        parts = sb("parts", [P, 3, 3, T], BF16)
        rest = sb("rest", [P, T])
        v_next = sb("v_next", [P, NT, D])
        v_sb = sb("v_sb", [P, NT, NH, STRIP])
        scratch = nc.dram_tensor("parts_dram", [3, NH, len(STORED), HD, T], BF16).ap()
        stack = sb("stack", [STACK, 3, NH, T], BF16)

        neg_max = sb("neg_max", [P, 2, QUAD, 2])
        sums = sb("sums", [P, 4, 2, QUAD])
        inv_l2 = sb("inv_l2", [P, QUAD])
        lam_l1 = sb("lam_l1", [P, QUAD])
        coef = sb("coef", [P, 2, QUAD])
        exps = sb("exps", [P, 2, 2, QUAD, T])
        diff = exps[:, :, 1, :, :]
        diffT = sb("diffT", [P, 2, QUAD, T])
        abs_sum = sb("abs_sum", [P, 2, QUAD])
        guard = sb("guard", [P, QUAD])
        inv_den = sb("inv_den", [P, NT, NH])
        inv_wide = sb("inv_wide", [P, NT, NH, HD])
        denT = sb("denT", [P, T])

        x_res = sb("x_res", [P, NT, D])
        attnT = sb("attnT", [P, T])
        r1 = sb("r1", [P, NT, D])
        x1 = sb("x1", [P, NT, D])
        xh = sb("xh", [P, NT, D])
        xnT = sb("xnT", [P, T])
        stats = sb("stats", [P, 3, NT, 6])
        mv = sb("mv", [P, 3, NT, 2])
        var_eps = sb("var_eps", [P, 3, NT])
        rstd = sb("rstd", [P, 3, NT])
        route_in = sb("route_in", [P, NT, E])
        route_max = sb("route_max", [P, NT])
        route_exp = sb("route_exp", [P, NT, E])
        route_inv = sb("route_inv", [P, NT])
        probs = sb("probs", [P, NT, E])
        top = sb("top", [P, 2, NT])
        first = sb("first", [P, 2, NT])
        hit = sb("hit", [P, 4, NT, E])
        gates = sb("gates", [P, NT, E])
        tanh_sb = sb("tanh_sb", [P, 2, T])
        hT = sb("hT", [P, 2, NF, T])
        x1_twice = sb("x1_twice", [P, NT, D])
        acc = sb("acc", [P, NT, D])
        y_out = sb("y_out", [P, NT, D])

        scores = pb("scores", [P, 2, 2, 512])
        trans = pb("trans", [P, NT * P])
        heads = pb("heads", [P, T])
        side = [pb(f"side{n}", [P, 512]) for n in range(2)]

        CONSTS = 9 + E
        weights_in = ctx.enter_context(nc.semaphore("weights_in"))
        experts_in = ctx.enter_context(nc.semaphore("experts_in"))
        consts_made = ctx.enter_context(nc.semaphore("consts_made"))
        lam_spread = ctx.enter_context(nc.semaphore("lam_spread"))
        lam_exp = ctx.enter_context(nc.semaphore("lam_exp"))
        lam_done = ctx.enter_context(nc.semaphore("lam_done"))
        x_loaded = signal("x_loaded", 1, 16)
        prep_psum = signal("prep_psum", len(PREP_TASKS))
        xT_copied = signal("xT_copied", 1)
        hi_made = signal("hi_made", 3)
        rest_made = signal("rest_made", 3)
        mid_made = signal("mid_made", 3)
        lo_made = signal("lo_made", 3)
        parts_out = signal("parts_out", sum(PARTS_STORED), 16)
        stack_in = [signal(f"stack_in{g}", 3 * len(WINDOWS), 16) for g in range(NG)]
        v_evacuated = signal("v_evacuated", 1)
        v_copied = signal("v_copied", 1)
        score_done = signal("score_done", 2 * UNITS)
        max_done = signal("max_done", 2 * UNITS)
        exp_done = signal("exp_done", 2 * UNITS)
        coef_done = signal("coef_done", 3 * QUADS)
        scaled_done = signal("scaled_done", UNITS)
        diff_done = signal("diff_done", UNITS)
        abs_done = signal("abs_done", 2 * QUADS)
        trans_done = signal("trans_done", UNITS)
        diffT_copied = signal("diffT_copied", UNITS)
        pv_done = signal("pv_done", QUADS)
        den_done = signal("den_done", 2 * QUADS)
        res_loaded = signal("res_loaded", 1, 16)
        post_psum = signal("post_psum", 4)
        expert_psum = signal("expert_psum", E * (NF + NT))
        inv_spread = signal("inv_spread", 1)
        denT_copied = signal("denT_copied", 1)
        attnT_done = signal("attnT_done", 1)
        r1_done = signal("r1_done", 1)
        moments_done = signal("moments_done", 2)
        eps_added = signal("eps_added", 2)
        rstd_done = signal("rstd_done", 2)
        last_moments = signal("last_moments", 1)
        last_eps = signal("last_eps", 1)
        last_rstd = signal("last_rstd", 1)
        x1_done = signal("x1_done", 1)
        acc_set = signal("acc_set", 1)
        xh_done = signal("xh_done", 1)
        xnT_copied = signal("xnT_copied", 1)
        logit_step = signal("logit_step", 2)
        router_exp = signal("router_exp", 1)
        route_step = signal("route_step", ROUTE_STEPS)
        tanh_done = signal("tanh_done", E * NF)
        hidden_done = signal("hidden_done", E * NF)
        expert_done = signal("expert_done", E * NT)
        y_done = signal("y_done", 1)
        y_stored = signal("y_stored", 1, 16)

        def reader(task):
            name = task[1]
            return {
                "den_T": (denT_copied, 1), "out_proj": (r1_done, 1), "xn_T": (xnT_copied, 1),
                "logits": (logit_step, 2), "x_T": (xT_copied, 1), "values": (v_evacuated, 1),
                "proj": (rest_made, task[2] + 1) if name == "proj" else None,
                "hidden": (hidden_done, NF * task[2] + task[3] + 1) if name == "hidden" else None,
                "expert": (expert_done, NT * task[2] + task[3] + 1) if name == "expert" else None,
            }[name]

        order = []
        for slot in range(UNITS):
            order += [("late", t) for t in SIDE.get(slot + UNITS, []) if t[1] in PSUM_TASKS]
            order += [(t[0], t) for t in SIDE.get(slot, []) if t[1] in PSUM_TASKS]
        bank_of = {t: n % 2 for n, (_, t) in enumerate(order)}
        wide = side + [scores[:, i, k, :] for i in range(2) for k in range(2)]
        wide_bank = {}
        for batches in ({"late": B - 2, "post": B - 1}, {"late": B - 1}):
            for kind, t in order:
                if kind in batches:
                    wide_bank[batches[kind], t] = len(wide_bank) % len(wide)

        def bank_number(n, task):
            return wide_bank.get((n, task) if isinstance(n, int) else None, bank_of[task])

        psum_count = {}
        for tasks in (POST_TASKS, PREP_TASKS):
            for experts in (False, True):
                chosen = [t for t in tasks if t[1] in PSUM_TASKS and (t[1] in ("hidden", "expert")) == experts]
                for n, t in enumerate(chosen):
                    psum_count[t] = n + 1

        def psum_of(task):
            if task[1] in ("hidden", "expert"):
                return expert_psum
            return post_psum if task[0] == "post" else prep_psum

        def run(engine, body):
            body(-1, ("prep",))
            body(0, ("attention", "prep"))
            body(1, ("attention", "prep", "post"))
            with engine.Fori(2, B - 1) as b:
                body(b, ("attention", "prep", "post", "late"))
            body(B - 1, ("attention", "post", "late"))
            body(B, ("trail", "post", "late"))
            body(B + 1, ("late",))

        def units(b, stages, slot, lag):
            u = slot - lag
            if u >= 0:
                return [(b, u)] if "attention" in stages else []
            if "trail" in stages or ("attention" in stages and not (isinstance(b, int) and b == 0)):
                return [(b - 1, u + UNITS)]
            return []

        def task_bank(n, task):
            return wide[bank_number(n, task)] if task in bank_of else None

        def side_tasks(b, stages, slot, lag=0):
            if "late" in stages:
                for task in SIDE.get(slot - lag + UNITS, []):
                    yield task, b - 2, task_bank(b - 2, task)
            for task in SIDE.get(slot - lag, []):
                if task[0] in stages:
                    n = b + 1 if task[0] == "prep" else b - 1
                    yield task, n, task_bank(n, task)

        def tiles(ap):
            return ap.rearrange("p (t d) -> p t d", t=NT)

        block = ctx.enter_context(nc.Block())

        @block.sync
        def _(sp):
            for dst, src in ((wq_sb[:, 0, :], wqT), (wq_sb[:, 1, :], wk1T), (wq_sb[:, 2, :], wk2T),
                             (wv_sb[:, :], wvT), (wo_sb[:, :], woT), (rw_sb[:, :], rwT),
                             (gamma_col[:, :], gamma), (beta_col[:, :], beta), (lam_row[:, :], lam)):
                sp.dma_start(dst, src).then_inc(weights_in, 16)
            for s in signals:
                sp.sem_inc(s.sem, CREDIT)

            def rows(ap, b):
                return ap[b, :, :].rearrange("(t p) d -> p t d", p=P) if isinstance(b, int) else \
                    ap[bass.ds(b, 1), :, :].rearrange("o (t p) d -> p (o t) d", p=P)

            def body(b, stages):
                if "prep" in stages:
                    n = b + 1
                    sp.wait_ge(prep_psum.sem, prep_psum.after(n - 1, 1))
                    sp.dma_start(x_in[:, :, :], rows(x, n)).then_inc(x_loaded.sem, 16)
                if "post" in stages:
                    sp.wait_ge(r1_done.sem, r1_done.after(b - 2, 1))
                    sp.dma_start(x_res[:, :, :], rows(x, b - 1)).then_inc(res_loaded.sem, 16)
                if "prep" in stages:
                    if isinstance(b, int) and b == -1:
                        for dst, src in ((w1_sb[:, :, :], w1.rearrange("e d f -> d e f")),
                                         (w2_sb[:, :, :, :], w2.rearrange("e (n f) d -> f e n d", f=P))):
                            sp.dma_start(dst, src).then_inc(experts_in, 16)
                    for z in range(3):
                        sp.wait_ge(lo_made.sem, lo_made.after(n, z + 1))
                        for g in range(NG):
                            sp.wait_ge(stack_in[g].sem, stack_in[g].after(n - 1, 3 * len(WINDOWS)))
                        for slot, part in enumerate(STORED[:PARTS_STORED[z]]):
                            sp.dma_start(scratch[z, :, slot, :, :], parts[:, z, part, :]).then_inc(parts_out.sem, 16)
                    sp.wait_ge(parts_out.sem, parts_out.after(n, sum(PARTS_STORED)))
                    for g in range(NG):
                        sp.wait_ge(score_done.sem, score_done.after(n - 1, 2 * (g + 1) * QUAD * NT))
                        for z in range(3):
                            for i, window in enumerate(WINDOWS):
                                slot = window if z else 0
                                sp.dma_start(stack[3 * HD * i:3 * HD * (i + 1), z, g * QUAD:(g + 1) * QUAD, :],
                                             scratch[z, g:NH:NG, slot:slot + 3, :, :].rearrange("h s d t -> (s d) h t"))\
                                  .then_inc(stack_in[g].sem, 16)
                if "late" in stages:
                    sp.wait_ge(y_done.sem, y_done.after(b - 2, 1))
                    sp.dma_start(rows(out, b - 2), y_out[:, :, :]).then_inc(y_stored.sem, 16)

            run(sp, body)
            sp.wait_ge(y_stored.sem, y_stored.after(B - 1, 1))
            sp.wait_ge(parts_out.sem, parts_out.after(B - 1, sum(PARTS_STORED)))

        @block.gpsimd
        def _(pool):
            nc.gpsimd.memset(ident[:, :], 0.0).then_inc(consts_made, 1)
            nc.gpsimd.memset(causal_bf[:, :], 0.0).then_inc(consts_made, 1)
            nc.gpsimd.memset(ones_row[:, :], 1.0).then_inc(consts_made, 1)
            nc.gpsimd.memset(minus_half[:, :], -0.5).then_inc(consts_made, 1)
            nc.gpsimd.memset(eps_row[:, :], EPS).then_inc(consts_made, 1)
            for e in range(E):
                nc.gpsimd.memset(rank[:, :, e:e + 1], float(E - e)).then_inc(consts_made, 1)
            nc.gpsimd.memset(v_sb[:, :, :, :], 0.0).then_inc(consts_made, 1)
            pool.wait_ge(consts_made, CONSTS - 3)
            nc.gpsimd.affine_select(out=ident[:, :], in_=ident[:, :], compare_op=ALU.not_equal, fill=1.0,
                                    base=0, pattern=[[-1, P]], channel_multiplier=1).then_inc(consts_made, 1)
            nc.gpsimd.affine_select(out=causal_bf[:, :], in_=causal_bf[:, :], compare_op=ALU.is_ge, fill=MASKED,
                                    base=0, pattern=[[-1, P]], channel_multiplier=1).then_inc(consts_made, 1)
            pool.wait_ge(consts_made, CONSTS - 1)
            nc.gpsimd.tensor_copy(ident_bf[:, :], ident[:, :]).then_inc(consts_made, 1)

            def body(b, stages):
                for slot in range(UNITS):
                    for n, u in units(b, stages, slot, LAG_DIFF):
                        q, j = divmod(u, QUAD)
                        w = (tile_of(q) + 1) * P
                        pool.wait_ge(coef_done.sem, coef_done.after(n, 3 * (q + 1)))
                        nc.gpsimd.tensor_tensor(diff[:, q % 2, j, 0:w], exps[:, q % 2, 1, j, 0:w],
                                                coef[:, q % 2, j:j + 1].broadcast_to([P, w]), ALU.mult)\
                            .then_inc(scaled_done.sem, 1)
                        pool.wait_ge(scaled_done.sem, scaled_done.after(n, u + 1))
                        nc.gpsimd.tensor_tensor(diff[:, q % 2, j, 0:w], diff[:, q % 2, j, 0:w],
                                                exps[:, q % 2, 0, j, 0:w], ALU.subtract).then_inc(diff_done.sem, 1)
                    for task, n, bank in side_tasks(b, stages, slot, 2 * LAG_SIDE):
                        name = task[1]
                        if name == "proj":
                            z = task[2]
                            pool.wait_ge(mid_made.sem, mid_made.after(n, z + 1))
                            nc.gpsimd.tensor_tensor(parts[:, z, 2, :], rest[:, :], parts[:, z, 1, :],
                                                    ALU.subtract).then_inc(lo_made.sem, 1)
                        if name in ("out_proj", "norm1", "norm3"):
                            i = ("out_proj", "norm1", "norm3").index(name)
                            moments, added, done = (moments_done, eps_added, rstd_done) if i < 2 else \
                                (last_moments, last_eps, last_rstd)
                            k = i + 1 if i < 2 else 1
                            pool.wait_ge(moments.sem, moments.after(n, k))
                            nc.gpsimd.tensor_tensor(var_eps[:, i, :], mv[:, i, :, 1], eps_row[:, :], ALU.add)\
                                .then_inc(added.sem, 1)
                            pool.wait_ge(added.sem, added.after(n, k))
                            nc.gpsimd.tensor_tensor(rstd[:, i, :], var_eps[:, i, :], minus_half[:, :], ALU.pow)\
                                .then_inc(done.sem, 1)

            run(pool, body)

        @block.scalar
        def _(act):
            act.wait_ge(lam_spread, 1)
            nc.scalar.activation(lam_all[:, :], side[0][:, 0:NH], ACT.Exp, scale=-1.0).then_inc(lam_exp, 1)

            def body(b, stages):
                for slot in range(UNITS):
                    for k in range(2):
                        for n, u in units(b, stages, slot, LAG_EXP):
                            q, j = divmod(u, QUAD)
                            w = (tile_of(q) + 1) * P
                            if k == 0:
                                act.wait_ge(diff_done.sem, diff_done.after(n, u + 1 - 2 * QUAD))
                            else:
                                act.wait_ge(trans_done.sem, trans_done.after(n, u + 1 - 2 * QUAD))
                                act.wait_ge(abs_done.sem, abs_done.after(n, 2 * (q - 2) + j // 2 + 1))
                            act.wait_ge(max_done.sem, max_done.after(n, 2 * u + k + 1))
                            nc.scalar.activation(exps[:, q % 2, k, j, 0:w], scores[:, u % 2, k, 0:w],
                                                 ACT.Exp, bias=neg_max[:, q % 2, j, k:k + 1],
                                                 accum_out=sums[:, q % 4, k, j:j + 1]).then_inc(exp_done.sem, 1)
                        for n, u in units(b, stages, slot, LAG_COPY) if k == 0 else ():
                            q, j = divmod(u, QUAD)
                            w = (tile_of(q) + 1) * P
                            act.wait_ge(trans_done.sem, trans_done.after(n, u + 1))
                            act.wait_ge(pv_done.sem, pv_done.after(n, q - 1))
                            nc.scalar.activation(diffT[:, q % 2, j, 0:w], trans[:, 0:w], ACT.Copy)\
                                .then_inc(diffT_copied.sem, 1)
                    for task, n, bank in side_tasks(b, stages, slot):
                        name = task[1]
                        if name == "x_T":
                            act.wait_ge(psum_of(task).sem, psum_of(task).after(n, psum_count[task]))
                            act.wait_ge(prep_psum.sem, prep_psum.after(n - 1, len(PREP_TASKS)))
                            nc.scalar.activation(xT[:, :], bank[:, :], ACT.Copy).then_inc(xT_copied.sem, 1)
                        if name == "proj":
                            z = task[2]
                            act.wait_ge(psum_of(task).sem, psum_of(task).after(n, psum_count[task]))
                            act.wait_ge(parts_out.sem, parts_out.after(n - 1, sum(PARTS_STORED)))
                            nc.scalar.activation(parts[:, z, 0, :], bank[:, :], ACT.Copy,
                                                 scale=SCALE if z == 0 else 1.0).then_inc(hi_made.sem, 1)
                        if name == "values":
                            act.wait_ge(psum_of(task).sem, psum_of(task).after(n, psum_count[task]))
                            act.wait_ge(v_copied.sem, v_copied.after(n - 1, 1))
                            nc.scalar.activation(v_next[:, :, :], tiles(bank[:, :]), ACT.Copy)\
                                .then_inc(v_evacuated.sem, 1)
                        if name == "den_T":
                            act.wait_ge(psum_of(task).sem, psum_of(task).after(n, psum_count[task]))
                            nc.scalar.activation(denT[:, :], bank[:, :], ACT.Copy).then_inc(denT_copied.sem, 1)
                        if name == "xn_T":
                            act.wait_ge(psum_of(task).sem, psum_of(task).after(n, psum_count[task]))
                            act.wait_ge(expert_psum.sem, expert_psum.after(n - 1, psum_count[("post", "hidden", E - 1, NF - 1)]))
                            nc.scalar.activation(xnT[:, :], bank[:, :], ACT.Identity, bias=beta_col[:, 0:1],
                                                 scale=gamma_col[:, 0:1]).then_inc(xnT_copied.sem, 1)
                        if name == "router_exp":
                            act.wait_ge(logit_step.sem, logit_step.after(n, 2))
                            act.wait_ge(route_step.sem, route_step.after(n - 1, ROUTE_STEPS))
                            nc.scalar.activation(route_exp[:, :, :], route_in[:, :, :], ACT.Exp, scale=1.0 / TEMP)\
                                .then_inc(router_exp.sem, 1)
                        if name == "hidden":
                            i = NF * task[2] + task[3]
                            act.wait_ge(psum_of(task).sem, psum_of(task).after(n, psum_count[task]))
                            act.wait_ge(hidden_done.sem, hidden_done.after(n, i - 1))
                            nc.scalar.activation(tanh_sb[:, i % 2, :], bank[:, :], ACT.Tanh, scale=0.5)\
                                .then_inc(tanh_done.sem, 1)

            run(act, body)

        @block.vector
        def _(dve):
            dve.wait_ge(lam_exp, 1)
            nc.vector.tensor_scalar_add(lam_all[:, :], lam_all[:, :], 1.0).then_inc(lam_done, 1)
            dve.wait_ge(lam_done, 1)
            nc.vector.reciprocal(lam_all[:, :], lam_all[:, :]).then_inc(lam_done, 1)
            dve.wait_ge(lam_done, 2)
            dve.wait_ge(consts_made, CONSTS)

            def moments(n, i, src):
                for t in range(NT):
                    nc.vector.bn_stats(stats[:, i, t, :], src[:, t, :])
                nc.vector.drain()
                for t in range(NT):
                    last = nc.vector.bn_aggr(mv[:, i, t, :], stats[:, i, t, :])
                last.then_inc((moments_done if i < 2 else last_moments).sem, 1)

            def normalise(n, i, dst, src):
                if i < 2:
                    dve.wait_ge(rstd_done.sem, rstd_done.after(n, i + 1))
                else:
                    dve.wait_ge(last_rstd.sem, last_rstd.after(n, 1))
                for t in range(NT):
                    last = nc.vector.tensor_scalar(dst[:, t, :], src[:, t, :], mv[:, i, t, 0:1],
                                                   rstd[:, i, t:t + 1], ALU.subtract, ALU.mult)
                return last

            def route(b, stages, slot, place):
                k = ROUTE_PLACES * (slot - ROUTE_SLOT) + place
                if "post" not in stages or not 0 <= k < ROUTE_STEPS:
                    return
                n = b - 1

                def over_experts(a):
                    return a.unsqueeze(2).broadcast_to([P, NT, E])

                second = k >= 9
                left = (hit[:, 3, :, :] if second else probs[:, :, :])
                if k == 0:
                    dve.wait_ge(router_exp.sem, router_exp.after(n, 1))
                    i = nc.vector.tensor_reduce(route_inv[:, :], route_exp[:, :, :], AX.X, ALU.add)
                else:
                    dve.wait_ge(route_step.sem, route_step.after(n, k))
                if k == 1:
                    i = nc.vector.reciprocal(route_inv[:, :], route_inv[:, :])
                if k == 2:
                    i = nc.vector.tensor_tensor(probs[:, :, :], route_exp[:, :, :], over_experts(route_inv[:, :]), ALU.mult)
                if k in (3, 9):
                    i = nc.vector.tensor_reduce(top[:, second, :], left, AX.X, ALU.max)
                if k in (4, 10):
                    i = nc.vector.tensor_tensor(hit[:, 2, :, :], left, over_experts(top[:, second, :]), ALU.is_equal)
                if k in (5, 11):
                    i = nc.vector.tensor_tensor(hit[:, 2, :, :], hit[:, 2, :, :], rank[:, :, :], ALU.mult)
                if k in (6, 12):
                    i = nc.vector.tensor_reduce(first[:, second, :], hit[:, 2, :, :], AX.X, ALU.max)
                if k in (7, 13):
                    i = nc.vector.tensor_tensor(hit[:, second, :, :], rank[:, :, :], over_experts(first[:, second, :]),
                                                ALU.is_equal)
                if k == 8:
                    i = nc.vector.scalar_tensor_tensor(out=hit[:, 3, :, :], in0=hit[:, 0, :, :], scalar=-2.0,
                                                       in1=probs[:, :, :], op0=ALU.mult, op1=ALU.add)
                if k == 14:
                    i = nc.vector.tensor_tensor(hit[:, 2, :, :], hit[:, 0, :, :], hit[:, 1, :, :], ALU.add)
                if k == 15:
                    i = nc.vector.scalar_tensor_tensor(out=gates[:, :, :], in0=hit[:, 2, :, :], scalar=0.5,
                                                       in1=probs[:, :, :], op0=ALU.mult, op1=ALU.mult)
                i.then_inc(route_step.sem, 1)

            def body(b, stages):
                for slot in range(UNITS):
                    route(b, stages, slot, 0)
                    for n, u in units(b, stages, slot, LAG_DEN):
                        q, j = divmod(u, QUAD)
                        if j == QUAD - 1:
                            dve.wait_ge(abs_done.sem, abs_done.after(n, 2 * (q + 1)))
                            nc.vector.scalar_tensor_tensor(out=guard[:, :], in0=sums[:, q % 4, 0, :], scalar=DENOM_MIN,
                                                           in1=abs_sum[:, q % 2, :], op0=ALU.mult, op1=ALU.max)\
                                .then_inc(den_done.sem, 1)
                    for task, n, bank in side_tasks(b, stages, slot, LAG_SIDE):
                        name = task[1]
                        if name == "proj":
                            z = task[2]
                            dve.wait_ge(psum_of(task).sem, psum_of(task).after(n, psum_count[task]))
                            dve.wait_ge(hi_made.sem, hi_made.after(n, z + 1))
                            dve.wait_ge(lo_made.sem, lo_made.after(n, z))
                            nc.vector.scalar_tensor_tensor(out=rest[:, :], in0=bank[:, :],
                                                           scalar=SCALE if z == 0 else 1.0, in1=parts[:, z, 0, :],
                                                           op0=ALU.mult, op1=ALU.subtract).then_inc(rest_made.sem, 1)
                            dve.wait_ge(rest_made.sem, rest_made.after(n, z + 1))
                            nc.vector.tensor_copy(parts[:, z, 1, :], rest[:, :]).then_inc(mid_made.sem, 1)
                        if name == "spread":
                            dve.wait_ge(den_done.sem, den_done.after(n, 2 * QUADS))
                            dve.wait_ge(post_psum.sem, post_psum.after(n - 1, psum_count[("post", "den_T")]))
                            nc.vector.tensor_copy(inv_wide[:, :, :, :],
                                                  inv_den[:, :, :].unsqueeze(3).broadcast_to([P, NT, NH, HD]))\
                                .then_inc(inv_spread.sem, 1)
                        if name == "divide":
                            dve.wait_ge(denT_copied.sem, denT_copied.after(n, 1))
                            dve.wait_ge(pv_done.sem, pv_done.after(n, QUADS))
                            nc.vector.scalar_tensor_tensor(out=attnT[:, :], in0=heads[:, :], scalar=-1.0,
                                                           in1=denT[:, :], op0=ALU.mult, op1=ALU.mult)\
                                .then_inc(attnT_done.sem, 1)
                        if name == "out_proj":
                            dve.wait_ge(psum_of(task).sem, psum_of(task).after(n, psum_count[task]))
                            dve.wait_ge(res_loaded.sem, res_loaded.after(n, 1))
                            nc.vector.tensor_tensor(r1[:, :, :], tiles(bank[:, :]), x_res[:, :, :], ALU.add)\
                                .then_inc(r1_done.sem, 1)
                            dve.wait_ge(r1_done.sem, r1_done.after(n, 1))
                            moments(n, 0, r1)
                        if name == "norm1":
                            normalise(n, 0, x1, r1).then_inc(x1_done.sem, 1)
                            dve.wait_ge(x1_done.sem, x1_done.after(n, 1))
                            moments(n, 1, x1)
                        if name == "norm2":
                            nc.vector.tensor_scalar(x1_twice[:, :, :], x1[:, :, :], 2.0, None, ALU.mult)\
                                .then_inc(acc_set.sem, 1)
                            normalise(n, 1, xh, x1).then_inc(xh_done.sem, 1)
                        if name == "logits":
                            dve.wait_ge(psum_of(task).sem, psum_of(task).after(n, psum_count[task]))
                            logits = bank[:, 0:NT * E].rearrange("p (t e) -> p t e", t=NT)
                            nc.vector.tensor_reduce(route_max[:, :], logits, AX.X, ALU.max)\
                                .then_inc(logit_step.sem, 1)
                            dve.wait_ge(logit_step.sem, logit_step.after(n, 1))
                            nc.vector.tensor_tensor(route_in[:, :, :], logits,
                                                    route_max[:, :].unsqueeze(2).broadcast_to([P, NT, E]),
                                                    ALU.subtract).then_inc(logit_step.sem, 1)
                        if name == "hidden":
                            e, f = task[2], task[3]
                            i = NF * e + f
                            dve.wait_ge(tanh_done.sem, tanh_done.after(n, i + 1))
                            m, used = (n, e - 2) if e >= 2 else (n - 1, e + E - 2)
                            used = ("post", "expert", used, NT - 1)
                            dve.wait_ge(expert_psum.sem, expert_psum.after(m, psum_count[used]))
                            nc.vector.scalar_tensor_tensor(out=hT[:, e % 2, f, :], in0=tanh_sb[:, i % 2, :],
                                                           scalar=1.0, in1=bank[:, :], op0=ALU.add, op1=ALU.mult)\
                                .then_inc(hidden_done.sem, 1)
                        if name == "expert":
                            e, t = task[2], task[3]
                            dve.wait_ge(psum_of(task).sem, psum_of(task).after(n, psum_count[task]))
                            if e == 0:
                                dve.wait_ge(route_step.sem, route_step.after(n, ROUTE_STEPS))
                                dve.wait_ge(acc_set.sem, acc_set.after(n, 1))
                            else:
                                dve.wait_ge(expert_done.sem, expert_done.after(n, NT * (e - 1) + t + 1))
                            nc.vector.scalar_tensor_tensor(
                                out=acc[:, t, :], in0=bank[:, 0:D], scalar=gates[:, t, e:e + 1],
                                in1=(acc if e else x1_twice)[:, t, :], op0=ALU.mult, op1=ALU.add).then_inc(expert_done.sem, 1)
                        if name == "norm3":
                            dve.wait_ge(expert_done.sem, expert_done.after(n, NT * E))
                            moments(n, 2, acc)
                        if name == "finish":
                            dve.wait_ge(y_stored.sem, y_stored.after(n - 1, 1))
                            normalise(n, 2, y_out, acc).then_inc(y_done.sem, 1)
                    for n, u in units(b, stages, slot, LAG_DIFF):
                        q, j = divmod(u, QUAD)
                        if j:
                            continue
                        dve.wait_ge(exp_done.sem, exp_done.after(n, 2 * (u + QUAD)))
                        nc.vector.reciprocal(inv_l2[:, :], sums[:, q % 4, 1, :]).then_inc(coef_done.sem, 1)
                        nc.vector.tensor_tensor(lam_l1[:, :], sums[:, q % 4, 0, :], lam_all[:, q // NT:NH:NG], ALU.mult)\
                            .then_inc(coef_done.sem, 1)
                        dve.wait_ge(diff_done.sem, diff_done.after(n, u - QUAD))
                        dve.wait_ge(coef_done.sem, coef_done.after(n, 3 * q + 2))
                        nc.vector.tensor_tensor(coef[:, q % 2, :], lam_l1[:, :], inv_l2[:, :], ALU.mult)\
                            .then_inc(coef_done.sem, 1)
                    route(b, stages, slot, 1)
                    for n, u in units(b, stages, slot, 0):
                        q, j = divmod(u, QUAD)
                        w = (tile_of(q) + 1) * P
                        dve.wait_ge(exp_done.sem, exp_done.after(n, 2 * (u + 1 - 2 * QUAD)))
                        for k in range(2):
                            dve.wait_ge(score_done.sem, score_done.after(n, 2 * u + k + 1))
                            nc.vector.tensor_reduce(neg_max[:, q % 2, j, k:k + 1], scores[:, u % 2, k, 0:w], AX.X,
                                                    ALU.max, negate=True).then_inc(max_done.sem, 1)
                    route(b, stages, slot, 2)
                    route(b, stages, slot, 3)
                    for n, u in units(b, stages, slot, LAG_ABS):
                        q, j = divmod(u, QUAD)
                        if j % 2 == 0:
                            continue
                        w = (tile_of(q) + 1) * P
                        dve.wait_ge(diff_done.sem, diff_done.after(n, u + 1))
                        nc.vector.tensor_reduce(abs_sum[:, q % 2, j - 1:j + 1], diff[:, q % 2, j - 1:j + 1, 0:w], AX.X,
                                                ALU.add, apply_absolute_value=True).then_inc(abs_done.sem, 1)
                    for n, u in units(b, stages, slot, LAG_DEN):
                        q, j = divmod(u, QUAD)
                        if j == QUAD - 1:
                            dve.wait_ge(den_done.sem, den_done.after(n, 2 * q + 1))
                            nc.vector.reciprocal(inv_den[:, tile_of(q), q // NT:NH:NG], guard[:, :])\
                                .then_inc(den_done.sem, 1)
                    if slot == LAG_PV and "attention" in stages:
                        dve.wait_ge(v_evacuated.sem, v_evacuated.after(b, 1))
                        dve.wait_ge(pv_done.sem, pv_done.after(b - 1, QUADS))
                        for g in range(NG):
                            last = nc.vector.tensor_copy(
                                v_sb[:, :, g:NH:NG, g * HD:(g + 1) * HD],
                                v_next[:, :, :].rearrange("p t (h d) -> p t h d", d=HD)[:, :, g:NH:NG, :])
                        last.then_inc(v_copied.sem, 1)

            run(dve, body)

        @block.tensor
        def _(pe):
            pe.wait_ge(weights_in, 9 * 16)
            pe.wait_ge(consts_made, CONSTS)
            nc.tensor.matmul(side[0][:, 0:NH], ones_row[:, :], lam_row[:, :], start=True, stop=True)\
                .then_inc(lam_spread, 1)
            pe.wait_ge(lam_done, 2)

            def side_task(task, n, bank, waits):
                name = task[1]
                for s, m, k in waits:
                    pe.wait_ge(s.sem, s.after(m, k))
                if name == "x_T":
                    pe.wait_ge(x_loaded.sem, x_loaded.after(n, 1))
                    for t in range(NT):
                        last = nc.tensor.transpose(bank[:, t * P:(t + 1) * P], x_in[:, t, :], ident[:, :])
                if name == "proj":
                    pe.wait_ge(xT_copied.sem, xT_copied.after(n, 1))
                    last = nc.tensor.matmul(bank[:, :], wq_sb[:, task[2], :], xT[:, :], start=True, stop=True)
                if name == "values":
                    pe.wait_ge(xT_copied.sem, xT_copied.after(n, 1))
                    for t in range(NT):
                        last = nc.tensor.matmul(bank[:, t * P:(t + 1) * P], xT[:, t * P:(t + 1) * P], wv_sb[:, :],
                                                start=True, stop=True)
                if name == "den_T":
                    pe.wait_ge(inv_spread.sem, inv_spread.after(n, 1))
                    for t in range(NT):
                        last = nc.tensor.transpose(bank[:, t * P:(t + 1) * P],
                                                   inv_wide[:, t, :, :].rearrange("p h d -> p (h d)"), ident[:, :])
                if name == "out_proj":
                    pe.wait_ge(attnT_done.sem, attnT_done.after(n, 1))
                    for t in range(NT):
                        last = nc.tensor.matmul(bank[:, t * P:(t + 1) * P], attnT[:, t * P:(t + 1) * P], wo_sb[:, :],
                                                start=True, stop=True)
                if name == "xn_T":
                    pe.wait_ge(xh_done.sem, xh_done.after(n, 1))
                    for t in range(NT):
                        last = nc.tensor.transpose(bank[:, t * P:(t + 1) * P], xh[:, t, :], ident[:, :])
                if name == "logits":
                    pe.wait_ge(xnT_copied.sem, xnT_copied.after(n, 1))
                    for t in range(NT):
                        last = nc.tensor.matmul(bank[:, t * E:(t + 1) * E], xnT[:, t * P:(t + 1) * P], rw_sb[:, :],
                                                start=True, stop=True)
                if name == "hidden":
                    e, f = task[2], task[3]
                    if isinstance(n, int) and n == 0 and e == f == 0:
                        pe.wait_ge(experts_in, 2 * 16)
                    pe.wait_ge(xnT_copied.sem, xnT_copied.after(n, 1))
                    last = nc.tensor.matmul(bank[:, :], w1_sb[:, e, f * P:(f + 1) * P], xnT[:, :],
                                            start=True, stop=True)
                if name == "expert":
                    e, t = task[2], task[3]
                    pe.wait_ge(hidden_done.sem, hidden_done.after(n, NF * (e + 1)))
                    for f in range(NF):
                        last = nc.tensor.matmul(bank[:, 0:D], hT[:, e % 2, f, t * P:(t + 1) * P],
                                                w2_sb[:, e, f, :], start=(f == 0), stop=(f == NF - 1))
                last.then_inc(psum_of(task).sem, 1)

            def bank_waits(b, stages):
                def batch(kind, b):
                    return b + {"prep": 1, "post": -1, "late": -2}[kind]

                last = {}
                before = [(b - 1, kind, t) for kind, t in order]
                if isinstance(b, int) and b == B + 1:
                    before = [(B - 1, kind, t) for kind, t in order] + \
                        [(B, kind, t) for kind, t in order if kind != "prep"]
                for m, kind, t in before:
                    last.setdefault(bank_number(batch(kind, m), t), {})[kind] = (t, batch(kind, m))
                found = {}
                for kind, t in order:
                    if kind not in stages:
                        continue
                    number = bank_number(batch(kind, b), t)
                    waits = []
                    for p, m in last.get(number, {}).values():
                        m = min(m, B - 1) if isinstance(m, int) else m
                        if not (isinstance(m, int) and m < 0):
                            waits.append((*reader(p)[:1], m, reader(p)[1]))
                    if number not in last:
                        waits.append((exp_done, B - 1, 2 * UNITS))
                    found[t] = waits
                    last[number] = {kind: (t, batch(kind, b))}
                return found

            def body(b, stages):
                waits = bank_waits(b, stages)
                for slot in range(UNITS):
                    for n, u in units(b, stages, slot, 0):
                        q, j = divmod(u, QUAD)
                        g, t = q // NT, tile_of(q)
                        w = (t + 1) * P
                        if q % NT == 0 and j == 0:
                            pe.wait_ge(stack_in[g].sem, stack_in[g].after(n, 3 * len(WINDOWS)))
                        for k in range(2):
                            pe.wait_ge(exp_done.sem, exp_done.after(n, 2 * (u - 2) + k + 1))
                            nc.tensor.matmul(scores[:, u % 2, k, 0:w], stack[:, 0, QUAD * g + j, t * P:(t + 1) * P],
                                             stack[:, 1 + k, QUAD * g + j, 0:w], start=True, stop=False)
                            nc.tensor.matmul(scores[:, u % 2, k, w - P:w], ident_bf[:, :], causal_bf[:, :],
                                             start=False, stop=True).then_inc(score_done.sem, 1)
                    for task, n, bank in side_tasks(b, stages, slot):
                        if task in bank_of:
                            side_task(task, n, bank, waits[task])
                    for n, u in units(b, stages, slot, LAG_PV):
                        q, j = divmod(u, QUAD)
                        g, t = q // NT, tile_of(q)
                        i = j - (QUAD - 1 - t)
                        if i < 0:
                            continue
                        if q == 0:
                            pe.wait_ge(v_copied.sem, v_copied.after(n, 1))
                            pe.wait_ge(attnT_done.sem, attnT_done.after(n - 1, 1))
                        pe.wait_ge(diffT_copied.sem, diffT_copied.after(n, QUAD * (q + 1)))
                        for k in range(QUAD):
                            last = nc.tensor.matmul(
                                heads[k * STRIP:(k + 1) * STRIP, t * P:(t + 1) * P], v_sb[:, i, NG * k + g, :],
                                diffT[:, q % 2, k, i * P:(i + 1) * P],
                                start=(q == 0 and i == 0), stop=(g == NG - 1 and i == t), skip_group_check=True)
                        if i == t:
                            last.then_inc(pv_done.sem, 1)
                    for n, u in units(b, stages, slot, LAG_TRANS):
                        q, j = divmod(u, QUAD)
                        pe.wait_ge(diff_done.sem, diff_done.after(n, u + 1))
                        pe.wait_ge(diffT_copied.sem, diffT_copied.after(n, u))
                        for i in range(tile_of(q) + 1):
                            last = nc.tensor.transpose(trans[:, i * P:(i + 1) * P],
                                                       diff[:, q % 2, j, i * P:(i + 1) * P], ident[:, :])
                        last.then_inc(trans_done.sem, 1)

            run(pe, body)


def kernel(**inputs):
    import numpy as np
    import concourse.bacc as bacc
    from concourse.bass_utils import run_bass_kernel_spmd

    a = {k.removeprefix("L0_"): np.asarray(v) for k, v in inputs.items()}
    laid = {
        "x": a["attn_x"], "wqT": a["attn_Wq"].T, "wk1T": a["attn_Wk1"].T, "wk2T": a["attn_Wk2"].T,
        "wvT": a["attn_Wv"].T, "woT": a["attn_Wo"].T, "lam": a["attn_lambda_logit"].reshape(1, NH),
        "gamma": a["ffn_gamma"].reshape(D, 1), "beta": a["ffn_beta"].reshape(D, 1),
        "rwT": a["ffn_router_w"].T, "w1": a["ffn_W1"], "w2": a["ffn_W2"],
    }
    nc = bacc.Bacc("TRN2", target_bir_lowering=False, num_devices=1)
    arrays, args = {}, []
    for name, value in laid.items():
        arrays[f"{name}_dram"] = np.ascontiguousarray(value)
        args.append(nc.dram_tensor(f"{name}_dram", value.shape, FP32, kind="ExternalInput").ap())
    args.append(nc.dram_tensor("o_dram", (B, T, D), FP32, kind="ExternalOutput").ap())
    build(nc, *args)
    r = run_bass_kernel_spmd(nc, [arrays], core_ids=[0])
    return r.results[0]["o_dram"]
```
